# Optimizing a Trainium2 kernel written in Bass

```python
import numpy as np
import jax
import jax.numpy as jnp

def _softmax(x, axis=-1):
    return jax.nn.softmax(x, axis=axis)

def _gelu(x):
    return jax.nn.gelu(x, approximate=True)

def _silu(x):
    return jax.nn.silu(x)

def _sigmoid(x):
    return jax.nn.sigmoid(x)

def _layernorm(x, axis=-1, eps=1e-05):
    m = jnp.mean(x, axis=axis, keepdims=True)
    v = jnp.var(x, axis=axis, keepdims=True)
    return (x - m) / jnp.sqrt(v + eps)

def _scatter_add(tgt, idx, src, axis=0):
    return tgt.at[idx].add(src)

def _segment_sum(src, seg, n):
    return jax.ops.segment_sum(src, seg, n)
kernel_name = 'mk_cond_resid_d2_seqx_r4_bf2331'

def setup_inputs(seed: int=0):
    np.random.seed(seed)
    _w = jnp.asarray

    def _rec_inputs():
        import jax
        import jax.numpy as jnp
        _rk = jax.random.key(seed)
        x = 7.22e-05 + 1 * jax.random.normal(jax.random.fold_in(_rk, 1), (8, 256, 1024), jnp.float32)
        _lenS = 256 - jax.random.randint(jax.random.fold_in(_rk, 7), (8,), 0, max(1, 256 // 4) + 1, jnp.int32)
        _lenS2 = 256 - jax.random.randint(jax.random.fold_in(_rk, 8), (8,), 0, max(1, 256 // 4) + 1, jnp.int32)
        condB_coeff = 0.00219231 + 0.0100837 * jax.random.normal(jax.random.fold_in(_rk, 11), (8,), jnp.float32)
        itok_B_2_6 = jax.random.randint(jax.random.fold_in(_rk, 13), (8,), 2, 7, jnp.int32)
        _validS = jnp.arange(256)[None, :] < _lenS[:, None]
        _validS2 = jnp.arange(256)[None, :] < _lenS2[:, None]
        _causal = jnp.tril(jnp.ones((256, 256), dtype=bool))
        mask_Bx4096x4096_ik1 = jnp.where(jnp.ones((8, 1024, 1024), dtype=bool), 1, 0).astype(jnp.int32)
        return (x, condB_coeff, itok_B_2_6, mask_Bx4096x4096_ik1)
    x, condB_coeff, itok_B_2_6, mask_Bx4096x4096_ik1 = _rec_inputs()

    def _L0_cond_setup():
        import jax, jax.numpy as jnp
        import numpy as np
        B, S, D_IN, D_OUT = (4, 128, 1024, 1024)
        key = jax.random.key(seed)
        k1, k2, k3, k4, k5 = jax.random.split(key, 5)
        hidden_states = jax.random.normal(k1, (B, S, D_IN), dtype=jnp.float32)
        W = jax.random.normal(k2, (D_OUT, D_IN), dtype=jnp.float32) * 0.02
        b = jax.random.normal(k3, (D_OUT,), dtype=jnp.float32) * 0.02
        coeff = jax.random.normal(k4, (B,), dtype=jnp.float32) * 0.01
        mask = jax.random.randint(k5, (B, D_IN, D_OUT), 0, 2, dtype=jnp.int32)
        return {'hidden_states': hidden_states, 'W': W, 'b': b, 'coeff': coeff, 'mask': mask}
    _L0_cond_all = _L0_cond_setup()
    _L0_cond_in = {k: v for k, v in _L0_cond_all.items() if k in ('W', 'b')}
    del _L0_cond_all

    def _L1_cond_setup():
        import jax, jax.numpy as jnp
        import numpy as np
        B, N, H, F = (4, 128, 1024, 2752)
        L, R, RANK = (1, 16, 16)
        SCALE = 0.5
        key = jax.random.key(seed)
        ks = jax.random.split(key, 12)
        nrm = lambda k, shape, fan: jax.random.normal(k, shape, jnp.float32) * fan ** (-0.5)
        inp = {'x': jax.random.normal(ks[0], (B, N, H), jnp.float32), 'W_gate': nrm(ks[1], (F, H), H), 'W_up': nrm(ks[2], (F, H), H), 'W_down': nrm(ks[3], (H, F), F), 'A_gate': nrm(ks[4], (L, R, RANK, H), H), 'B_gate': nrm(ks[5], (L, R, F, RANK), RANK), 'A_up': nrm(ks[6], (L, R, RANK, H), H), 'B_up': nrm(ks[7], (L, R, F, RANK), RANK), 'A_down': nrm(ks[8], (L, R, RANK, F), F), 'B_down': nrm(ks[9], (L, R, H, RANK), RANK), 'lora_indices': jax.random.randint(ks[10], (B,), 0, R), 'layer_idx': 0}
        return inp
    _L1_cond_all = _L1_cond_setup()
    _L1_cond_in = {k: v for k, v in _L1_cond_all.items() if k in ('W_gate', 'W_up', 'W_down', 'A_gate', 'B_gate', 'A_up', 'B_up', 'A_down', 'B_down')}
    del _L1_cond_all
    return {'x': x, 'condB_coeff': condB_coeff, 'itok_B_2_6': itok_B_2_6, 'mask_Bx4096x4096_ik1': mask_Bx4096x4096_ik1, 'L0_cond_W': _L0_cond_in['W'], 'L0_cond_b': _L0_cond_in['b'], 'L1_cond_W_gate': _L1_cond_in['W_gate'], 'L1_cond_W_up': _L1_cond_in['W_up'], 'L1_cond_W_down': _L1_cond_in['W_down'], 'L1_cond_A_gate': _L1_cond_in['A_gate'], 'L1_cond_B_gate': _L1_cond_in['B_gate'], 'L1_cond_A_up': _L1_cond_in['A_up'], 'L1_cond_B_up': _L1_cond_in['B_up'], 'L1_cond_A_down': _L1_cond_in['A_down'], 'L1_cond_B_down': _L1_cond_in['B_down']}

def reference(x, condB_coeff, itok_B_2_6, mask_Bx4096x4096_ik1, L0_cond_W, L0_cond_b, L1_cond_W_gate, L1_cond_W_up, L1_cond_W_down, L1_cond_A_gate, L1_cond_B_gate, L1_cond_A_up, L1_cond_B_up, L1_cond_A_down, L1_cond_B_down):
    import jax
    import jax.numpy as jnp

    def _L0_cond_ref(hidden_states, W, b, coeff, mask):
        import jax, jax.numpy as jnp
        import numpy as np
        B, S, D_IN, D_OUT = (4, 128, 1024, 1024)
        output = jnp.einsum('bsi,oi->bso', hidden_states, W) + b
        sign = (2 * mask - 1).astype(hidden_states.dtype)
        diff = jnp.einsum('bsi,bio->bso', hidden_states, sign)
        return output + diff * coeff[:, None, None]

    def _L1_cond_ref(x, W_gate, W_up, W_down, A_gate, B_gate, A_up, B_up, A_down, B_down, lora_indices, layer_idx):
        import jax, jax.numpy as jnp
        import numpy as np
        B, N, H, F = (4, 128, 1024, 2752)
        L, R, RANK = (1, 16, 16)
        SCALE = 0.5

        def lora_add(base, inp, A, B):
            Ab = A[layer_idx][lora_indices]
            Bb = B[layer_idx][lora_indices]
            t = jnp.einsum('bri,bni->bnr', Ab, inp)
            return base + jnp.einsum('bor,bnr->bno', Bb, t) * SCALE
        gate = lora_add(jnp.einsum('bnh,fh->bnf', x, W_gate), x, A_gate, B_gate)
        up = lora_add(jnp.einsum('bnh,fh->bnf', x, W_up), x, A_up, B_up)
        act = jax.nn.silu(gate) * up
        down = lora_add(jnp.einsum('bnf,hf->bnh', act, W_down), act, A_down, B_down)
        return down
    x = x + _L0_cond_ref(x, L0_cond_W, L0_cond_b, condB_coeff, mask_Bx4096x4096_ik1)
    x = x + _L1_cond_ref(x, L1_cond_W_gate, L1_cond_W_up, L1_cond_W_down, L1_cond_A_gate, L1_cond_B_gate, L1_cond_A_up, L1_cond_B_up, L1_cond_A_down, L1_cond_B_down, itok_B_2_6, 0)
    return x

_drawn_inputs = setup_inputs


def setup_inputs(seed=0):
    import zlib

    import numpy as np

    out = dict(_drawn_inputs(seed))
    spreads = {}
    factors = {'L0_cond_b': 2.909}
    for name, (base, spread) in spreads.items():
        noise = np.random.default_rng([zlib.crc32(name.encode()), seed]).standard_normal(out[name].shape)
        drawn = base * np.exp(spread * noise) if base else spread * noise
        out[name] = jnp.asarray(drawn.astype(out[name].dtype))
    for name, factor in factors.items():
        out[name] = (out[name] * factor).astype(out[name].dtype)
    return out
```

```python
from contextlib import ExitStack

import numpy as np

import concourse.bass as bass
from concourse import mybir

P = 128
B, S, H, F, ADAPTERS, RANK = 8, 256, 1024, 2752, 16, 16
LORA_SCALE = 0.5
BLOCKS, PAIR = 4, 2
T = PAIR * S
HT = H // P
FT = -(-F // P)
SEGS = [8, 8, 6]
SEG_AT = [0, 8, 16]
RING = 4
S0 = HT * PAIR
GU_AT, DN_AT, _at = [], [], S0
for _n in SEGS:
    GU_AT.append(_at)
    DN_AT.append(_at + 2 * _n)
    _at += 2 * _n + HT
CHUNKS = _at
TURNS = CHUNKS // RING
R2 = PAIR * RANK
COPIES = 3


def build(nc, x, mask, coeff, w0, bias, wgu, wd, a_gate, a_up, a_down, b_gu, b_down, idx, ident, own, out):
    f32, f32r, i32 = mybir.dt.float32, mybir.dt.float32r, mybir.dt.int32
    ACT, ALU = mybir.ActivationFunctionType, mybir.AluOpType
    ds = bass.ds

    def row(t, i):
        if isinstance(i, int):
            return t[:, i, :]
        return t[:, ds(i, 1), :].rearrange("p a n -> p (a n)")

    def next_block(blk):
        return nc.s_assert_within(blk + 1, 1, BLOCKS - 1, skip_runtime_bounds_check_because="the branch is taken before the last block only")

    def turn(blk, at, it):
        return TURNS * blk + at // RING + it

    with ExitStack() as ctx:
        def sb(name, shape, dt):
            return ctx.enter_context(nc.sbuf_tensor(name, shape, dt))

        def ps(name):
            return ctx.enter_context(nc.psum_tensor(name, [P, T], f32))

        def sem(name):
            return ctx.enter_context(nc.semaphore(name))

        def sems(name, n):
            return [sem(f"{name}{i}") for i in range(n)]

        raw = sb("raw", [P, RING, H], f32)
        raw_i = raw[:, :, :].bitcast(i32)
        hi = sb("hi", [P, RING, H], f32r)
        lo = sb("lo", [P, RING, H], f32r)
        w_in = sb("w_in", [P, 2, H], f32)
        xh = sb("xh", [P, HT, T], f32r)
        xl = sb("xl", [P, HT, T], f32r)
        x1 = sb("x1", [P, HT, T], f32)
        x1h = sb("x1h", [P, HT, T], f32r)
        x1l = sb("x1l", [P, HT, T], f32r)
        acth = sb("acth", [P, max(SEGS), T], f32r)
        actl = sb("actl", [P, max(SEGS), T], f32r)
        work = sb("work", [P, 2, T], f32)
        stage = sb("stage", [P, 2, T], f32)
        b_in = sb("b_in", [COPIES * R2, 2, max(SEGS) * P], f32)
        bd_in = sb("bd_in", [COPIES * R2, H], f32)
        b_w = sb("b_w", [COPIES * R2, RING, P], f32r)
        a_in = sb("a_in", [P, 2 * PAIR, HT, RANK], f32)
        a_w = sb("a_w", [P, HT, 4 * R2], f32r)
        ad_in = sb("ad_in", [P, PAIR, max(SEGS), RANK], f32)
        ad_w = sb("ad_w", [P, max(SEGS), 2 * R2], f32r)
        t_gate = sb("t_gate", [COPIES * R2, T], f32r)
        t_up = sb("t_up", [COPIES * R2, T], f32r)
        t_down = sb("t_down", [COPIES * R2, T], f32r)
        own_sb = sb("own_sb", [2 * R2, T], f32)
        ident_sb = sb("ident_sb", [P, P], f32)
        bias_sb = sb("bias_sb", [P, HT], f32)
        coeff_sb = sb("coeff_sb", [P, B], f32)
        coeff2 = sb("coeff2", [P, B], f32)
        ncoeff = sb("ncoeff", [P, B], f32)
        idx_sb = sb("idx_sb", [1, B], i32)

        gate_ps = [ps("gate_ps0"), ps("gate_ps1")]
        up_ps = [ps("up_ps0"), ps("up_ps1")]
        down_ps = [ps("down_ps0"), ps("down_ps1")]
        ta_ps = ps("ta_ps")
        td_ps = ps("td_ps")

        consts_in = sem("consts_in")
        idx_in = sem("idx_in")
        coeffs_ready = sem("coeffs_ready")
        x_in = sems("x_in", 2)
        xh_ready = sems("xh_ready", 2)
        xl_ready = sems("xl_ready", 2)
        w_loaded = sems("w_loaded", 2)
        w_ident = sems("w_ident", 2)
        raw_loaded = sems("raw_loaded", RING)
        sign_ready = sems("sign_ready", RING)
        wc_ready = sems("wc_ready", RING)
        hi_ready = sems("hi_ready", RING)
        lo_ready = sems("lo_ready", RING)
        chunk_used = sems("chunk_used", RING)
        x1h_ready = sems("x1h_ready", 2)
        x1l_ready = sem("x1l_ready")
        a_loaded = sem("a_loaded")
        ah_ready = sem("ah_ready")
        al_ready = sem("al_ready")
        ad_loaded = sem("ad_loaded")
        adh_ready = sem("adh_ready")
        adl_ready = sem("adl_ready")
        b_loaded = sem("b_loaded")
        bd_loaded = sem("bd_loaded")
        t_done = sem("t_done")
        t_low = sem("t_low")
        t_sum = sem("t_sum")
        t_own = sem("t_own")
        t_hi = sem("t_hi")
        t_ready = sem("t_ready")
        silu_ready = sem("silu_ready")
        gu_read = sems("gu_read", 2)
        acth_ready = sem("acth_ready")
        act_ready = sem("act_ready")
        down_read = sems("down_read", 2)
        out_stored = sems("out_stored", 2)

        block = ctx.enter_context(nc.Block())

        @block.sync
        def _(sp):
            def met():
                sp.wait_ge(idx_in, 16)

            def load_x(blk, k, acts=0):
                met()
                sp.wait_ge(xl_ready[k % 2], (HT // 2) * blk + k // 2)
                if not isinstance(acts, int):
                    sp.wait_ge(act_ready, acts)
                sp.dma_start(work[:, k % 2, :], x[ds(blk * HT + k, 1), :, :].rearrange("a p n -> p (a n)")
                             ).then_inc(x_in[k % 2], 16)

            def load_chunk(blk, at, it, u, src):
                met()
                sp.wait_ge(lo_ready[u], turn(blk, at, it))
                sp.dma_start(raw[:, u, 0:src.shape[-1]], src).then_inc(raw_loaded[u], 16)

            def load_stage0(blk, it, u):
                if u % 2 == 0:
                    o, par = 2 * it + u // 2, u // 2
                    met()
                    sp.wait_ge(wc_ready[u + 1], (HT // 2) * blk + it)
                    sp.dma_start(w_in[:, par, :], w0[ds(o, 1), :, :].rearrange("a p n -> p (a n)")
                                 ).then_inc(w_loaded[par], 16)
                c = S0 * blk + 4 * it + u
                met()
                sp.wait_ge(lo_ready[u], turn(blk, 0, it))
                sp.dma_start(raw_i[:, u, :], mask[ds(c, 1), :, :].rearrange("a p n -> p (a n)")
                             ).then_inc(raw_loaded[u], 16)

            def load_a_down(seg, adapter):
                for b in range(PAIR):
                    src = a_down[ds(adapter[b], 1), :, SEG_AT[seg] * RANK:(SEG_AT[seg] + SEGS[seg]) * RANK]
                    sp.dma_start(ad_in[:, b, 0:SEGS[seg], :].rearrange("p k r -> p (k r)"),
                                 src.rearrange("a p n -> p (a n)")).then_inc(ad_loaded, 16)

            def load_b_gu(seg, adapter):
                lo_f, n = SEG_AT[seg] * P, SEGS[seg] * P
                for q in range(COPIES):
                    for b in range(PAIR):
                        r = q * R2 + b * RANK
                        sp.dma_start(b_in[r:r + RANK, :, 0:n],
                                     b_gu[ds(adapter[b], 1), :, :, lo_f:lo_f + n].rearrange("a r g n -> (a r) g n")
                                     ).then_inc(b_loaded, 16)

            sp.dma_start(idx_sb[:, :], idx).then_inc(idx_in, 16)
            sp.dma_start(coeff_sb[:, :], coeff).then_inc(consts_in, 16)
            sp.dma_start(bias_sb[:, :], bias).then_inc(consts_in, 16)
            sp.dma_start(ident_sb[:, :], ident).then_inc(consts_in, 16)
            load_x(0, 0)
            load_x(0, 1)
            load_stage0(0, 0, 0)
            for k in range(2, HT):
                load_x(0, k)
            for u in range(1, RING):
                load_stage0(0, 0, u)
            sp.dma_start(own_sb[:, :], own).then_inc(consts_in, 16)
            sp.wait_ge(idx_in, 16)
            with sp.Fori(0, BLOCKS) as blk:
                adapter = [sp.value_load(idx_sb[0:1, ds(PAIR * blk + b, 1)], min_val=0, max_val=ADAPTERS - 1)
                           for b in range(PAIR)]
                for m, a in enumerate((a_gate, a_up)):
                    for b in range(PAIR):
                        sp.dma_start(a_in[:, PAIR * m + b, :, :].rearrange("p k r -> p (k r)"),
                                     a[ds(adapter[b], 1), :, :].rearrange("a p n -> p (a n)")).then_inc(a_loaded, 16)
                load_a_down(0, adapter)
                load_b_gu(0, adapter)
                with sp.Fori(1, S0 // RING) as it:
                    for u in range(RING):
                        load_stage0(blk, it, u)
                for q in range(COPIES):
                    for b in range(PAIR):
                        r = q * R2 + b * RANK
                        sp.dma_start(bd_in[r:r + RANK, :],
                                     b_down[ds(adapter[b], 1), :, :].rearrange("a r n -> (a r) n")
                                     ).then_inc(bd_loaded, 16)
                for seg, n in enumerate(SEGS):
                    with sp.Fori(0, 2 * n // RING) as it:
                        for u in range(RING):
                            c = 2 * SEG_AT[seg] + 4 * it + u
                            load_chunk(blk, GU_AT[seg], it, u,
                                       wgu[ds(c, 1), :, :].rearrange("a p n -> p (a n)"))
                    with sp.Fori(0, HT // RING) as it:
                        for u in range(RING):
                            cols = slice(SEG_AT[seg] * P, (SEG_AT[seg] + n) * P)
                            load_chunk(blk, DN_AT[seg], it, u,
                                       wd[ds(4 * it + u, 1), :, cols].rearrange("a p n -> p (a n)"))
                    if seg + 1 < len(SEGS):
                        load_a_down(seg + 1, adapter)
                        load_b_gu(seg + 1, adapter)
                with sp.If(blk < BLOCKS - 1):
                    after = next_block(blk)
                    load_x(after, 0, acts=FT * blk + FT)
                    load_x(after, 1)
                    for u in range(RING):
                        load_stage0(after, 0, u)
                        load_x(after, 2 + u)
                    load_x(after, 6)
                    load_x(after, 7)

        @block.scalar
        def _(act):
            def copy(o, i):
                return nc.scalar.activation(o, i, ACT.Copy)

            def met():
                act.wait_ge(coeffs_ready, 1)

            def split_x(blk, k):
                act.wait_ge(x_in[k % 2], 16 * ((HT // 2) * blk + k // 2 + 1))
                copy(xh[:, k, :], work[:, k % 2, :]).then_inc(xh_ready[k % 2], 1)

            def form_sign(blk, it, u):
                b = PAIR * blk + u % 2
                met()
                act.wait_ge(raw_loaded[u], 16 * (turn(blk, 0, it) + 1))
                nc.scalar.activation(raw[:, u, :], raw_i[:, u, :], ACT.Identity, bias=ncoeff[:, ds(b, 1)],
                                     scale=coeff2[:, ds(b, 1)]).then_inc(sign_ready[u], 1)

            def split_stage0(blk, it, u):
                act.wait_ge(wc_ready[u], (S0 // RING) * blk + it + 1)
                act.wait_ge(chunk_used[u], turn(blk, 0, it))
                copy(hi[:, u, :], raw[:, u, :]).then_inc(hi_ready[u], 1)

            def split_gu(blk, seg, it, u):
                f = 2 * it + u // 2
                met()
                act.wait_ge(chunk_used[u], turn(blk, GU_AT[seg], it))
                copy(b_w[:, u, :], b_in[:, u % 2, ds(f * P, P)])
                act.wait_ge(raw_loaded[u], 16 * (turn(blk, GU_AT[seg], it) + 1))
                copy(hi[:, u, :], raw[:, u, :]).then_inc(hi_ready[u], 1)

            def split_down(blk, seg, it, u):
                n = SEGS[seg] * P
                met()
                act.wait_ge(chunk_used[u], turn(blk, DN_AT[seg], it))
                if seg == len(SEGS) - 1:
                    h = 4 * it + u
                    copy(b_w[:, u, :], bd_in[:, ds(h * P, P)])
                act.wait_ge(raw_loaded[u], 16 * (turn(blk, DN_AT[seg], it) + 1))
                copy(hi[:, u, 0:n], raw[:, u, 0:n]).then_inc(hi_ready[u], 1)

            def finish_x1(blk, it, u):
                if u % 2 == 0:
                    return
                o, par = 2 * it + u // 2, u // 2
                met()
                act.wait_ge(chunk_used[u], turn(blk, 0, it) + 1)
                nc.scalar.activation(row(x1, o), gate_ps[par][:, :], ACT.Identity, bias=bias_sb[:, ds(o, 1)])
                nc.scalar.activation(row(x1h, o), gate_ps[par][:, :], ACT.Identity, bias=bias_sb[:, ds(o, 1)]
                                     ).then_inc(x1h_ready[par], 1)

            def form_t(blk, which, src, rows, parts):
                act.wait_ge(t_done, 2 * blk + which + 1)
                for par in range(2):
                    act.wait_ge(out_stored[par], 16 * (HT // 2) * blk)
                copy(stage[0:rows, 0, :], src[rows:2 * rows, :]).then_inc(t_low, 1)
                act.wait_ge(t_own, 2 * blk + which + 1)
                for dst, r in parts:
                    copy(dst[0:R2, :], stage[r:r + R2, 1, :])
                    last = copy(dst[R2:2 * R2, :], stage[r:r + R2, 1, :])
                last.then_inc(t_hi, 1)

            act.wait_ge(coeffs_ready, 1)
            for k in range(2):
                split_x(0, k)
            form_sign(0, 0, 0)
            for k in range(2, HT):
                split_x(0, k)
            for u in range(RING):
                form_sign(0, *divmod(u + 1, RING))
                split_stage0(0, 0, u)

            with act.Fori(0, BLOCKS) as blk:
                def stage0_step(it, u):
                    if u == RING - 1:
                        act.wait_ge(raw_loaded[0], 16 * (turn(blk, 0, it + 2) + 1))
                    finish_x1(blk, it, u)
                    form_sign(blk, it + 1 + (u + 1) // RING, (u + 1) % RING)
                    split_stage0(blk, it + 1, u)

                with act.Fori(0, S0 // RING - 2) as it:
                    for u in range(RING):
                        stage0_step(it, u)
                it = S0 // RING - 2
                for u in range(RING - 1):
                    stage0_step(it, u)
                finish_x1(blk, it, RING - 1)
                split_stage0(blk, it + 1, RING - 1)
                act.wait_ge(a_loaded, 16 * 2 * PAIR * (blk + 1))
                copy(a_w[:, :, 0:2 * R2].rearrange("p k (m r) -> p k m r", r=RANK),
                     a_in[:, :, :, :].rearrange("p m k r -> p k m r")).then_inc(ah_ready, 1)
                for u in range(RING):
                    if u == 0:
                        act.wait_ge(b_loaded, 16 * COPIES * PAIR * (len(SEGS) * blk + 1))
                    finish_x1(blk, S0 // RING - 1, u)
                    split_gu(blk, 0, 0, u)
                form_t(blk, 0, ta_ps, 2 * R2, [(t_gate, 0), (t_up, R2)])

                for seg, n in enumerate(SEGS):
                    def finish_act(it, u, then):
                        if u % 2 == 0:
                            return then()
                        f, par = 2 * it + u // 2, u // 2
                        act.wait_ge(chunk_used[u], turn(blk, GU_AT[seg], it) + 1)
                        nc.scalar.activation(work[:, 0, :], gate_ps[par][:, :], ACT.Silu).then_inc(silu_ready, 1)
                        then()
                        met()
                        act.wait_ge(gu_read[par], (FT // 2) * blk + SEG_AT[seg] // 2 + it + 1)
                        copy(row(acth, f), work[:, 1, :]).then_inc(acth_ready, 1)

                    with act.Fori(0, 2 * n // RING - 1) as it:
                        for u in range(RING):
                            finish_act(it, u, lambda: split_gu(blk, seg, it + 1, u))
                    act.wait_ge(ad_loaded, 16 * PAIR * (len(SEGS) * blk + seg + 1))
                    copy(ad_w[:, 0:n, 0:R2].rearrange("p k (b r) -> p k b r", r=RANK),
                         ad_in[:, :, 0:n, :].rearrange("p b k r -> p k b r")).then_inc(adh_ready, 1)
                    if seg == len(SEGS) - 1:
                        act.wait_ge(bd_loaded, 16 * COPIES * PAIR * (blk + 1))
                    for u in range(RING):
                        finish_act(2 * n // RING - 1, u, lambda: split_down(blk, seg, 0, u))

                    if seg < len(SEGS) - 1:
                        for u in range(RING):
                            split_down(blk, seg, 1, u)
                        act.wait_ge(b_loaded, 16 * COPIES * PAIR * (len(SEGS) * blk + seg + 2))
                        for u in range(RING):
                            split_gu(blk, seg + 1, 0, u)
                    else:
                        form_t(blk, 1, td_ps, R2, [(t_down, 0)])

                        def store(h):
                            par = h % 2
                            act.wait_ge(down_read[par], (3 * HT // 2) * blk + HT + h // 2 + 1)
                            act.dma_start(out[ds(HT * blk + h, 1), :, :].rearrange("a p n -> p (a n)"),
                                          stage[:, par, :]).then_inc(out_stored[par], 16)

                        more = blk < BLOCKS - 1
                        for u in range(RING):
                            with act.If(more):
                                split_x(blk + 1, u)
                            split_down(blk, seg, 1, u)
                            store(u)
                        for u in range(RING):
                            with act.If(more):
                                after = next_block(blk)
                                split_x(after, RING + u)
                                if u == 0:
                                    form_sign(after, 0, 0)
                                form_sign(after, *divmod(u + 1, RING))
                                split_stage0(after, 0, u)
                            store(RING + u)
            for par in range(2):
                act.wait_ge(out_stored[par], 16 * (HT // 2) * BLOCKS)

        @block.vector
        def _(dve):
            def sub(o, a, b):
                return nc.vector.tensor_tensor(o, a, b, ALU.subtract)

            def add(o, a, b):
                return nc.vector.tensor_tensor(o, a, b, ALU.add)

            def split_x(blk, k):
                dve.wait_ge(xh_ready[k % 2], (HT // 2) * blk + k // 2 + 1)
                sub(xl[:, k, :], work[:, k % 2, :], xh[:, k, :]).then_inc(xl_ready[k % 2], 1)

            def form_matrix(blk, it, u):
                o, par = 2 * it + u // 2, u // 2
                n = (HT // 2) * blk + it
                if u % 2 == 0:
                    dve.wait_ge(w_loaded[par], 16 * (n + 1))
                    tile = w_in[:, par, ds(o * P, P)]
                    add(tile, tile, ident_sb[:, :]).then_inc(w_ident[par], 1)
                    dve.wait_ge(w_ident[par], n + 1)
                dve.wait_ge(sign_ready[u], n + 1)
                add(raw[:, u, :], raw[:, u, :], w_in[:, par, :]).then_inc(wc_ready[u], 1)

            def split_stage0(blk, it, u):
                dve.wait_ge(hi_ready[u], turn(blk, 0, it) + 1)
                sub(lo[:, u, :], raw[:, u, :], hi[:, u, :]).then_inc(lo_ready[u], 1)

            def split_gu(blk, seg, it, u):
                f = 2 * it + u // 2
                dve.wait_ge(hi_ready[u], turn(blk, GU_AT[seg], it) + 1)
                q = slice(R2, 2 * R2)
                sub(b_w[q, u, :], b_in[q, u % 2, ds(f * P, P)], b_w[q, u, :])
                sub(lo[:, u, :], raw[:, u, :], hi[:, u, :]).then_inc(lo_ready[u], 1)

            def split_down(blk, seg, it, u):
                n = SEGS[seg] * P
                dve.wait_ge(hi_ready[u], turn(blk, DN_AT[seg], it) + 1)
                if seg == len(SEGS) - 1:
                    h = 4 * it + u
                    q = slice(R2, 2 * R2)
                    sub(b_w[q, u, :], bd_in[q, ds(h * P, P)], b_w[q, u, :])
                sub(lo[:, u, 0:n], raw[:, u, 0:n], hi[:, u, 0:n]).then_inc(lo_ready[u], 1)

            def finish_x1(blk, it, u):
                if u % 2 == 0:
                    return
                o, par = 2 * it + u // 2, u // 2
                dve.wait_ge(x1h_ready[par], (HT // 2) * blk + it + 1)
                sub(row(x1l, o), row(x1, o), row(x1h, o)).then_inc(x1l_ready, 1)

            def form_t(blk, which, src, rows, parts):
                n = 2 * blk + which + 1
                dve.wait_ge(t_low, n)
                t = stage[0:rows, 1, :]
                add(t, src[0:rows, :], stage[0:rows, 0, :]).then_inc(t_sum, 1)
                dve.wait_ge(t_sum, n)
                nc.vector.tensor_tensor(t, t, own_sb[0:rows, :], ALU.mult).then_inc(t_own, 1)
                dve.wait_ge(t_hi, n)
                for dst, r in parts:
                    last = sub(dst[2 * R2:3 * R2, :], stage[r:r + R2, 1, :], dst[r:r + R2, :])
                last.then_inc(t_ready, 1)

            dve.wait_ge(consts_in, 16 * 3)
            nc.vector.tensor_scalar(coeff2[:, :], coeff_sb[:, :], 2.0, None, ALU.mult)
            nc.vector.tensor_scalar(ncoeff[:, :], coeff_sb[:, :], -1.0, None, ALU.mult).then_inc(coeffs_ready, 1)
            for k in range(2):
                split_x(0, k)
            form_matrix(0, 0, 0)
            for k in range(2, HT):
                split_x(0, k)
            for u in range(RING):
                form_matrix(0, *divmod(u + 1, RING))
                split_stage0(0, 0, u)
            dve.wait_ge(consts_in, 16 * 4)

            with dve.Fori(0, BLOCKS) as blk:
                def stage0_step(it, u):
                    finish_x1(blk, it, u)
                    form_matrix(blk, it + 1 + (u + 1) // RING, (u + 1) % RING)
                    split_stage0(blk, it + 1, u)

                with dve.Fori(0, S0 // RING - 2) as it:
                    for u in range(RING):
                        stage0_step(it, u)
                it = S0 // RING - 2
                for u in range(RING - 1):
                    stage0_step(it, u)
                finish_x1(blk, it, RING - 1)
                split_stage0(blk, it + 1, RING - 1)
                dve.wait_ge(ah_ready, blk + 1)
                sub(a_w[:, :, 2 * R2:4 * R2].rearrange("p k (m r) -> p k m r", r=RANK),
                    a_in[:, :, :, :].rearrange("p m k r -> p k m r"),
                    a_w[:, :, 0:2 * R2].rearrange("p k (m r) -> p k m r", r=RANK)).then_inc(al_ready, 1)
                for u in range(RING):
                    finish_x1(blk, S0 // RING - 1, u)
                    split_gu(blk, 0, 0, u)
                form_t(blk, 0, ta_ps, 2 * R2, [(t_gate, 0), (t_up, R2)])

                for seg, n in enumerate(SEGS):
                    def finish_act(it, u, then):
                        if u % 2 == 0:
                            return then()
                        f, par = 2 * it + u // 2, u // 2
                        done = FT * blk + SEG_AT[seg] + f + 1
                        dve.wait_ge(act_ready, done - 1)
                        dve.wait_ge(silu_ready, done)
                        nc.vector.tensor_tensor(work[:, 1, :], work[:, 0, :], up_ps[par][:, :], ALU.mult
                                                ).then_inc(gu_read[par], 1)
                        then()
                        dve.wait_ge(acth_ready, done)
                        sub(row(actl, f), work[:, 1, :], row(acth, f)).then_inc(act_ready, 1)

                    with dve.Fori(0, 2 * n // RING - 1) as it:
                        for u in range(RING):
                            finish_act(it, u, lambda: split_gu(blk, seg, it + 1, u))
                    dve.wait_ge(adh_ready, len(SEGS) * blk + seg + 1)
                    sub(ad_w[:, 0:n, R2:2 * R2].rearrange("p k (b r) -> p k b r", r=RANK),
                        ad_in[:, :, 0:n, :].rearrange("p b k r -> p k b r"),
                        ad_w[:, 0:n, 0:R2].rearrange("p k (b r) -> p k b r", r=RANK)).then_inc(adl_ready, 1)
                    for u in range(RING):
                        finish_act(2 * n // RING - 1, u, lambda: split_down(blk, seg, 0, u))

                    def finish_down(h):
                        par = h % 2
                        dve.wait_ge(chunk_used[h % RING], turn(blk, DN_AT[seg], h // RING) + 1)
                        if seg:
                            dve.wait_ge(down_read[par], (3 * HT // 2) * blk + (HT // 2) * (seg - 1) + h // 2 + 1)
                        if seg < len(SEGS) - 1:
                            dst = x1[:, h, :]
                        else:
                            dve.wait_ge(out_stored[par], 16 * ((HT // 2) * blk + h // 2))
                            dst = stage[:, par, :]
                        add(dst, x1[:, h, :], down_ps[par][:, :]).then_inc(down_read[par], 1)

                    if seg < len(SEGS) - 1:
                        for u in range(RING):
                            finish_down(u)
                            split_down(blk, seg, 1, u)
                        for u in range(RING):
                            finish_down(RING + u)
                            split_gu(blk, seg + 1, 0, u)
                    else:
                        form_t(blk, 1, td_ps, R2, [(t_down, 0)])
                        more = blk < BLOCKS - 1
                        for u in range(RING):
                            finish_down(u)
                            with dve.If(more):
                                split_x(blk + 1, u)
                            split_down(blk, seg, 1, u)
                        for u in range(RING):
                            finish_down(RING + u)
                            with dve.If(more):
                                split_x(blk + 1, RING + u)
                                if u == 0:
                                    form_matrix(blk + 1, 0, 0)
                                form_matrix(blk + 1, *divmod(u + 1, RING))
                                split_stage0(blk + 1, 0, u)

        @block.tensor
        def _(pe):
            mm = nc.tensor.matmul

            def three(dst, u, k, vh, vl, first, last, lora=None):
                w = slice(k * P, (k + 1) * P)
                mm(dst, hi[:, u, w], vh, start=first, stop=False)
                mm(dst, hi[:, u, w], vl, start=False, stop=False)
                if last and lora is not None:
                    mm(dst, b_w[:, u, :], lora[:, :], start=False, stop=False)
                end = mm(dst, lo[:, u, w], vh, start=False, stop=last)
                if last:
                    end.then_inc(chunk_used[u], 1)

            with pe.Fori(0, BLOCKS) as blk:
                with pe.Fori(0, S0 // RING) as it:
                    for par in range(2):
                        pe.wait_ge(xl_ready[par], (HT // 2) * (blk + 1))
                    for u in range(RING):
                        b, par = u % 2, u // 2
                        if b == 0:
                            pe.wait_ge(x1h_ready[par], (HT // 2) * blk + it)
                        pe.wait_ge(lo_ready[u], turn(blk, 0, it) + 1)
                        cols = slice(b * S, (b + 1) * S)
                        for k in range(HT):
                            three(gate_ps[par][:, cols], u, k, xh[:, k, cols], xl[:, k, cols], k == 0, k == HT - 1)

                pe.wait_ge(al_ready, blk + 1)
                for k in range(HT):
                    if k == 0 or k == HT - 1:
                        pe.wait_ge(x1l_ready, HT * blk + (HT if k else HT - 1))
                    mm(ta_ps[:, :], a_w[:, k, :], x1h[:, k, :], start=k == 0, stop=False)
                    end = mm(ta_ps[:, :], a_w[:, k, :], x1l[:, k, :], start=False, stop=k == HT - 1)
                end.then_inc(t_done, 1)

                for seg, n in enumerate(SEGS):
                    with pe.Fori(0, 2 * n // RING) as it:
                        for u in range(RING):
                            par = u // 2
                            if u % 2 == 0:
                                pe.wait_ge(gu_read[par], (FT // 2) * blk + SEG_AT[seg] // 2 + it)
                            pe.wait_ge(lo_ready[u], turn(blk, GU_AT[seg], it) + 1)
                            dst, t = ((gate_ps[par], t_gate), (up_ps[par], t_up))[u % 2]
                            for k in range(HT):
                                if k == HT - 1 and seg == 0:
                                    pe.wait_ge(t_ready, 2 * blk + 1)
                                three(dst[:, :], u, k, x1h[:, k, :], x1l[:, k, :], k == 0, k == HT - 1, t)

                    pe.wait_ge(adl_ready, len(SEGS) * blk + seg + 1)
                    for k in range(n):
                        if k == 0 or k == n - 1:
                            pe.wait_ge(act_ready, FT * blk + SEG_AT[seg] + (n if k else n - 1))
                        start, stop = seg == 0 and k == 0, seg == len(SEGS) - 1 and k == n - 1
                        mm(td_ps[0:2 * R2, :], ad_w[:, k, :], acth[:, k, :], start=start, stop=False)
                        end = mm(td_ps[0:2 * R2, :], ad_w[:, k, :], actl[:, k, :], start=False, stop=stop)
                    if seg == len(SEGS) - 1:
                        end.then_inc(t_done, 1)
                    with pe.Fori(0, HT // RING) as it:
                        for u in range(RING):
                            par = u % 2
                            pe.wait_ge(down_read[par], (3 * HT // 2) * blk + (HT // 2) * seg + 2 * it + u // 2)
                            pe.wait_ge(lo_ready[u], turn(blk, DN_AT[seg], it) + 1)
                            for k in range(n):
                                lora = t_down if seg == len(SEGS) - 1 else None
                                if lora is not None and k == n - 1:
                                    pe.wait_ge(t_ready, 2 * blk + 2)
                                three(down_ps[par][:, :], u, k, acth[:, k, :], actl[:, k, :], k == 0, k == n - 1, lora)


def kernel(x, condB_coeff, itok_B_2_6, mask_Bx4096x4096_ik1, L0_cond_W, L0_cond_b, L1_cond_W_gate, L1_cond_W_up,
           L1_cond_W_down, L1_cond_A_gate, L1_cond_B_gate, L1_cond_A_up, L1_cond_B_up, L1_cond_A_down,
           L1_cond_B_down):
    import concourse.bacc as bacc
    from concourse.bass_utils import run_bass_kernel_spmd

    FP = FT * P

    def pad_f(a, axis):
        widths = [(0, 0)] * a.ndim
        widths[axis] = (0, FP - F)
        return np.pad(a, widths)

    def tiles(w, n_out, n_in):
        return w.reshape(n_out, P, n_in, P).transpose(0, 3, 2, 1).reshape(n_out, P, n_in * P)

    x, mask = np.asarray(x), np.asarray(mask_Bx4096x4096_ik1)
    wg, wu = (tiles(pad_f(np.asarray(w), 0), FT, HT) for w in (L1_cond_W_gate, L1_cond_W_up))
    a_gate, a_up = (np.asarray(a)[0].reshape(ADAPTERS, RANK, HT, P).transpose(0, 3, 2, 1).reshape(ADAPTERS, P, -1)
                    for a in (L1_cond_A_gate, L1_cond_A_up))
    a_down = pad_f(np.asarray(L1_cond_A_down)[0], 2)
    a_down = a_down.reshape(ADAPTERS, RANK, FT, P).transpose(0, 3, 2, 1).reshape(ADAPTERS, P, -1)
    b_gate, b_up = (pad_f(np.asarray(b)[0].transpose(0, 2, 1), 2) for b in (L1_cond_B_gate, L1_cond_B_up))
    rows, cols = np.arange(2 * R2) % R2 // RANK, np.arange(T) // S
    arrays = {
        "x": x.reshape(BLOCKS, T, HT, P).transpose(0, 2, 3, 1).reshape(BLOCKS * HT, P, T),
        "mask": mask.reshape(BLOCKS, PAIR, HT, P, HT, P).transpose(0, 4, 1, 3, 2, 5).reshape(BLOCKS * S0, P, H),
        "coeff": np.broadcast_to(np.asarray(condB_coeff), (P, B)),
        "w0": tiles(np.asarray(L0_cond_W), HT, HT),
        "bias": np.asarray(L0_cond_b).reshape(HT, P).T,
        "wgu": np.stack([wg, wu], 1).reshape(2 * FT, P, H),
        "wd": tiles(pad_f(np.asarray(L1_cond_W_down), 1), HT, FT),
        "a_gate": a_gate, "a_up": a_up, "a_down": a_down,
        "b_gu": np.stack([b_gate, b_up], 2),
        "b_down": np.asarray(L1_cond_B_down)[0].transpose(0, 2, 1),
        "idx": np.asarray(itok_B_2_6).reshape(1, B),
        "ident": np.eye(P, dtype=np.float32),
        "own": np.where(rows[:, None] == cols[None, :], np.float32(LORA_SCALE), np.float32(0)),
    }
    arrays = {f"in_{k}": np.ascontiguousarray(v) for k, v in arrays.items()}
    nc = bacc.Bacc("TRN2", target_bir_lowering=False, num_devices=1)
    args = [nc.dram_tensor(k, v.shape, mybir.dt.from_np(v.dtype), kind="ExternalInput").ap() for k, v in arrays.items()]
    args.append(nc.dram_tensor("out", (BLOCKS * HT, P, T), mybir.dt.float32, kind="ExternalOutput").ap())
    build(nc, *args)
    got = run_bass_kernel_spmd(nc, [arrays], core_ids=[0]).results[0]["out"]
    return got.reshape(BLOCKS, H, T).transpose(0, 2, 1).reshape(B, S, H)
```

```python
from contextlib import ExitStack

import numpy as np

import concourse.bass as bass
from concourse import mybir

P = 128
B, S, H, F, ADAPTERS, RANK = 8, 256, 1024, 2752, 16, 16
LORA_SCALE = 0.5
BLOCKS, PAIR = 4, 2
T = PAIR * S
HT = H // P
FT = -(-F // P)
HALF = F % P
assert 2 * HALF == P
SEGS = [8, 8, 6]
SEG_AT = [0, 8, 16]
X_SEG = 1
RING = 4
S0 = HT * PAIR
GU_AT, DN_AT, _at = [], [], S0
for _n in SEGS:
    GU_AT.append(_at)
    DN_AT.append(_at + 2 * _n)
    _at += 2 * _n + HT
CHUNKS = _at
TURNS = CHUNKS // RING
R2 = PAIR * RANK
COPIES = 3


def build(nc, x, mask, coeff, w0, bias, wgu, wd, a_gate, a_up, a_down, b_gu, b_down, idx, ident, own, out):
    f32, f32r, i32 = mybir.dt.float32, mybir.dt.float32r, mybir.dt.int32
    ACT, ALU = mybir.ActivationFunctionType, mybir.AluOpType
    ds = bass.ds

    def row(t, i):
        if isinstance(i, int):
            return t[:, i, :]
        return t[:, ds(i, 1), :].rearrange("p a n -> p (a n)")

    def next_block(blk):
        return nc.s_assert_within(blk + 1, 1, BLOCKS - 1, skip_runtime_bounds_check_because="the branch is taken before the last block only")

    def is_half(seg, it, u):
        return seg == len(SEGS) - 1 and isinstance(it, int) and 2 * it + u // 2 == SEGS[seg] - 1

    def half_of(t, u):
        c = (u % 2) * HALF
        return t[:, u - u % 2, :].rearrange("p (k c) -> p k c", c=P)[:, :, c:c + HALF]

    def turn(blk, at, it):
        return TURNS * blk + at // RING + it

    with ExitStack() as ctx:
        def sb(name, shape, dt):
            return ctx.enter_context(nc.sbuf_tensor(name, shape, dt))

        def ps(name):
            return ctx.enter_context(nc.psum_tensor(name, [P, T], f32))

        def sem(name):
            return ctx.enter_context(nc.semaphore(name))

        def sems(name, n):
            return [sem(f"{name}{i}") for i in range(n)]

        raw = sb("raw", [P, RING, H], f32)
        raw_i = raw[:, :, :].bitcast(i32)
        hi = sb("hi", [P, RING, H], f32r)
        lo = sb("lo", [P, RING, H], f32r)
        w_in = sb("w_in", [P, 2, H], f32)
        xh = sb("xh", [P, HT, T], f32r)
        xl = sb("xl", [P, HT, T], f32r)
        x1 = sb("x1", [P, HT, T], f32)
        x1h = sb("x1h", [P, HT, T], f32r)
        x1l = sb("x1l", [P, HT, T], f32r)
        acth = sb("acth", [P, max(SEGS), T], f32r)
        actl = sb("actl", [P, max(SEGS), T], f32r)
        x_in = sb("x_in", [P, T], f32)
        work = sb("work", [P, 2, T], f32)
        stage = sb("stage", [P, 2, T], f32)
        b_in = sb("b_in", [COPIES * R2, 2, max(SEGS) * P], f32)
        bd_in = sb("bd_in", [COPIES * R2, H], f32)
        b_w = sb("b_w", [COPIES * R2, RING, P], f32r)
        a_in = sb("a_in", [P, 2 * PAIR, HT, RANK], f32)
        a_w = sb("a_w", [P, HT, 4 * R2], f32r)
        ad_in = sb("ad_in", [P, PAIR, max(SEGS), RANK], f32)
        ad_w = sb("ad_w", [P, max(SEGS), 2 * R2], f32r)
        t_gate = sb("t_gate", [COPIES * R2, T], f32r)
        t_up = sb("t_up", [COPIES * R2, T], f32r)
        t_down = t_gate
        own_sb = sb("own_sb", [2 * R2, T], f32)
        ident_sb = sb("ident_sb", [P, P], f32)
        bias_sb = sb("bias_sb", [P, HT], f32)
        coeff_sb = sb("coeff_sb", [P, B], f32)
        coeff2 = sb("coeff2", [P, B], f32)
        ncoeff = sb("ncoeff", [P, B], f32)
        silu_warm = sb("silu_warm", [P, 1], f32)
        idx_sb = sb("idx_sb", [1, B], i32)

        gate_ps = [ps("gate_ps0"), ps("gate_ps1")]
        up_ps = [ps("up_ps0"), ps("up_ps1")]
        down_ps = [ps("down_ps0"), ps("down_ps1")]
        ta_ps = ps("ta_ps")
        td_ps = ps("td_ps")

        consts_in = sem("consts_in")
        own_in = sem("own_in")
        idx_in = sem("idx_in")
        coeffs_ready = sem("coeffs_ready")
        x0_loaded = sems("x0_loaded", HT)
        x_loaded = sem("x_loaded")
        xh_ready = sem("xh_ready")
        xl_ready = sem("xl_ready")
        w_loaded = sems("w_loaded", 2)
        w_ident = sems("w_ident", 2)
        raw_loaded = sems("raw_loaded", RING)
        sign_ready = sems("sign_ready", RING)
        wc_ready = sems("wc_ready", RING)
        hi_ready = sems("hi_ready", RING)
        lo_ready = sems("lo_ready", RING)
        chunk_used = sems("chunk_used", RING)
        x1h_ready = sems("x1h_ready", 2)
        x1l_ready = sem("x1l_ready")
        a_loaded = sem("a_loaded")
        ah_ready = sem("ah_ready")
        al_ready = sem("al_ready")
        ad_loaded = sem("ad_loaded")
        adh_ready = sem("adh_ready")
        adl_ready = sem("adl_ready")
        b_loaded = sem("b_loaded")
        bd_loaded = sem("bd_loaded")
        t_done = sem("t_done")
        t_low = sem("t_low")
        t_sum = sem("t_sum")
        t_own = sem("t_own")
        t_hi = sem("t_hi")
        t_top = sem("t_top")
        t_ready = sem("t_ready")
        silu_ready = sem("silu_ready")
        gu_read = sems("gu_read", 2)
        acth_ready = sem("acth_ready")
        act_ready = sem("act_ready")
        down_read = sems("down_read", 2)
        out_stored = sems("out_stored", 2)

        block = ctx.enter_context(nc.Block())

        @block.sync
        def _(sp):
            def met():
                sp.wait_ge(idx_in, 16)

            def load_chunk(blk, at, it, u, src):
                met()
                sp.wait_ge(lo_ready[u], turn(blk, at, it))
                sp.dma_start(raw[:, u, 0:src.shape[-1]], src).then_inc(raw_loaded[u], 16)

            def load_stage0(blk, it, u):
                if u % 2 == 0:
                    o, par = 2 * it + u // 2, u // 2
                    met()
                    sp.wait_ge(wc_ready[u + 1], (HT // 2) * blk + it)
                    sp.dma_start(w_in[:, par, :], w0[ds(o, 1), :, :].rearrange("a p n -> p (a n)")
                                 ).then_inc(w_loaded[par], 16)
                c = S0 * blk + 4 * it + u
                met()
                sp.wait_ge(lo_ready[u], turn(blk, 0, it))
                sp.dma_start(raw_i[:, u, :], mask[ds(c, 1), :, :].rearrange("a p n -> p (a n)")
                             ).then_inc(raw_loaded[u], 16)

            sp.dma_start(idx_sb[:, :], idx).then_inc(idx_in, 16)
            sp.dma_start(coeff_sb[:, :], coeff).then_inc(consts_in, 16)
            sp.dma_start(bias_sb[:, :], bias).then_inc(consts_in, 16)
            sp.dma_start(ident_sb[:, :], ident).then_inc(consts_in, 16)
            load_stage0(0, 0, 0)
            for k in range(HT):
                sp.dma_start(x1[:, k, :], x[k, :, :]).then_inc(x0_loaded[k], 16)
            for u in range(1, RING):
                load_stage0(0, 0, u)
            sp.dma_start(own_sb[:, :], own).then_inc(own_in, 16)
            sp.wait_ge(idx_in, 16)
            with sp.Fori(0, BLOCKS) as blk:
                with sp.Fori(1, S0 // RING) as it:
                    for u in range(RING):
                        load_stage0(blk, it, u)
                for seg, n in enumerate(SEGS):
                    whole = 2 * n // RING - (seg == len(SEGS) - 1)
                    with sp.Fori(0, whole) as it:
                        for u in range(RING):
                            c = 2 * SEG_AT[seg] + 4 * it + u
                            load_chunk(blk, GU_AT[seg], it, u,
                                       wgu[ds(c, 1), :, :].rearrange("a p n -> p (a n)"))
                    if seg == len(SEGS) - 1:
                        for u in range(RING):
                            c = 2 * SEG_AT[seg] + 4 * whole + u
                            load_chunk(blk, GU_AT[seg], whole, u,
                                       wgu[c, :, :] if u < 2 else wgu[c, :, 0:H // 2])
                    with sp.Fori(0, HT // RING) as it:
                        for u in range(RING):
                            cols = slice(SEG_AT[seg] * P, (SEG_AT[seg] + n) * P)
                            load_chunk(blk, DN_AT[seg], it, u,
                                       wd[ds(4 * it + u, 1), :, cols].rearrange("a p n -> p (a n)"))
                with sp.If(blk < BLOCKS - 1):
                    after = next_block(blk)
                    for u in range(RING):
                        load_stage0(after, 0, u)

        @block.gpsimd
        def _(pool):
            def load_a_down(seg, adapter):
                for b in range(PAIR):
                    src = a_down[ds(adapter[b], 1), :, SEG_AT[seg] * RANK:(SEG_AT[seg] + SEGS[seg]) * RANK]
                    pool.dma_start(ad_in[:, b, 0:SEGS[seg], :].rearrange("p k r -> p (k r)"),
                                 src.rearrange("a p n -> p (a n)")).then_inc(ad_loaded, 16)

            def load_b_gu(seg, adapter):
                lo_f, n = SEG_AT[seg] * P, SEGS[seg] * P
                for q in range(COPIES):
                    for b in range(PAIR):
                        r = q * R2 + b * RANK
                        pool.dma_start(b_in[r:r + RANK, :, 0:n],
                                     b_gu[ds(adapter[b], 1), :, :, lo_f:lo_f + n].rearrange("a r g n -> (a r) g n")
                                     ).then_inc(b_loaded, 16)

            def adapters(blk):
                return [pool.value_load(idx_sb[0:1, ds(PAIR * blk + b, 1)], min_val=0, max_val=ADAPTERS - 1)
                        for b in range(PAIR)]

            def load_first(adapter):
                for m, a in enumerate((a_gate, a_up)):
                    for b in range(PAIR):
                        pool.dma_start(a_in[:, PAIR * m + b, :, :].rearrange("p k r -> p (k r)"),
                                       a[ds(adapter[b], 1), :, :].rearrange("a p n -> p (a n)")).then_inc(a_loaded, 16)
                load_a_down(0, adapter)
                load_b_gu(0, adapter)

            pool.wait_ge(idx_in, 16)
            pool.wait_ge(x0_loaded[HT - 1], 16)
            load_first(adapters(0))
            with pool.Fori(0, BLOCKS) as blk:
                adapter = adapters(blk)
                for seg in range(1, len(SEGS)):
                    pool.wait_ge(adl_ready, len(SEGS) * blk + seg)
                    pool.wait_ge(lo_ready[RING - 1], turn(blk, DN_AT[seg - 1], 0))
                    load_a_down(seg, adapter)
                    load_b_gu(seg, adapter)
                    if seg == X_SEG:
                        for q in range(COPIES):
                            for b in range(PAIR):
                                r = q * R2 + b * RANK
                                pool.dma_start(bd_in[r:r + RANK, :],
                                               b_down[ds(adapter[b], 1), :, :].rearrange("a r n -> (a r) n")
                                               ).then_inc(bd_loaded, 16)
                        with pool.If(blk < BLOCKS - 1):
                            after = next_block(blk)
                            with pool.Fori(0, HT) as k:
                                pool.wait_ge(xl_ready, HT * after + k)
                                pool.dma_start(x_in[:, :], x[ds(HT * after + k, 1), :, :].rearrange("a p n -> p (a n)")
                                               ).then_inc(x_loaded, 16)
                with pool.If(blk < BLOCKS - 1):
                    pool.wait_ge(adl_ready, len(SEGS) * (blk + 1))
                    pool.wait_ge(lo_ready[RING - 1], turn(blk, DN_AT[-1], 0))
                    load_first(adapters(next_block(blk)))

        @block.scalar
        def _(act):
            def copy(o, i):
                return nc.scalar.activation(o, i, ACT.Copy)

            def met():
                act.wait_ge(coeffs_ready, 1)

            def split_next_x(blk, k):
                act.wait_ge(x_loaded, 16 * (HT * blk + k + 1))
                copy(row(xh, k), x_in[:, :]).then_inc(xh_ready, 1)

            def form_sign(blk, it, u):
                b = PAIR * blk + u % 2
                met()
                act.wait_ge(raw_loaded[u], 16 * (turn(blk, 0, it) + 1))
                nc.scalar.activation(raw[:, u, :], raw_i[:, u, :], ACT.Identity, bias=ncoeff[:, ds(b, 1)],
                                     scale=coeff2[:, ds(b, 1)]).then_inc(sign_ready[u], 1)

            def split_stage0(blk, it, u):
                act.wait_ge(wc_ready[u], (S0 // RING) * blk + it + 1)
                act.wait_ge(chunk_used[u], turn(blk, 0, it))
                copy(hi[:, u, :], raw[:, u, :]).then_inc(hi_ready[u], 1)

            def split_gu(blk, seg, it, u):
                f = 2 * it + u // 2
                met()
                act.wait_ge(chunk_used[u], turn(blk, GU_AT[seg], it))
                copy(b_w[:, u, :], b_in[:, u % 2, ds(f * P, P)])
                act.wait_ge(raw_loaded[u], 16 * (turn(blk, GU_AT[seg], it) + 1))
                if is_half(seg, it, u):
                    copy(half_of(hi, u), raw[:, u, 0:H // 2].rearrange("p (k c) -> p k c", c=HALF)
                         ).then_inc(hi_ready[u], 1)
                else:
                    copy(hi[:, u, :], raw[:, u, :]).then_inc(hi_ready[u], 1)

            def split_down(blk, seg, it, u):
                n = SEGS[seg] * P
                met()
                act.wait_ge(chunk_used[u], turn(blk, DN_AT[seg], it))
                if seg == len(SEGS) - 1:
                    h = 4 * it + u
                    copy(b_w[:, u, :], bd_in[:, ds(h * P, P)])
                act.wait_ge(raw_loaded[u], 16 * (turn(blk, DN_AT[seg], it) + 1))
                copy(hi[:, u, 0:n], raw[:, u, 0:n]).then_inc(hi_ready[u], 1)

            def finish_x1(blk, it, u):
                if u % 2 == 0:
                    return
                o, par = 2 * it + u // 2, u // 2
                met()
                act.wait_ge(chunk_used[u], turn(blk, 0, it) + 1)
                nc.scalar.activation(row(x1, o), gate_ps[par][:, :], ACT.Identity, bias=bias_sb[:, ds(o, 1)])
                nc.scalar.activation(row(x1h, o), gate_ps[par][:, :], ACT.Identity, bias=bias_sb[:, ds(o, 1)]
                                     ).then_inc(x1h_ready[par], 1)

            def form_t(blk, which, src, rows, parts):
                act.wait_ge(t_done, 2 * blk + which + 1)
                for par in range(2):
                    act.wait_ge(out_stored[par], 16 * (HT // 2) * blk)
                copy(stage[0:rows, 0, :], src[rows:2 * rows, :]).then_inc(t_low, 1)
                act.wait_ge(t_own, 2 * blk + which + 1)
                for dst, r in parts:
                    copy(dst[R2:2 * R2, :], stage[r:r + R2, 1, :]).then_inc(t_hi, 1)

            act.wait_ge(coeffs_ready, 1)
            nc.scalar.activation(silu_warm[:, :], coeff_sb[:, 0:1], ACT.Silu)
            form_sign(0, 0, 0)
            for k in range(HT):
                act.wait_ge(x0_loaded[k], 16)
                copy(xh[:, k, :], x1[:, k, :]).then_inc(xh_ready, 1)
                if k == HT // 2 - 1:
                    split_stage0(0, 0, 0)
            form_sign(0, 0, 1)
            for u in range(1, RING):
                form_sign(0, *divmod(u + 1, RING))
                split_stage0(0, 0, u)

            with act.Fori(0, BLOCKS) as blk:
                def stage0_step(it, u):
                    if u == RING - 1:
                        act.wait_ge(raw_loaded[0], 16 * (turn(blk, 0, it + 2) + 1))
                    finish_x1(blk, it, u)
                    form_sign(blk, it + 1 + (u + 1) // RING, (u + 1) % RING)
                    split_stage0(blk, it + 1, u)

                with act.Fori(0, S0 // RING - 2) as it:
                    for u in range(RING):
                        stage0_step(it, u)
                it = S0 // RING - 2
                for u in range(RING - 1):
                    stage0_step(it, u)
                finish_x1(blk, it, RING - 1)
                split_stage0(blk, it + 1, RING - 1)
                act.wait_ge(a_loaded, 16 * 2 * PAIR * (blk + 1))
                copy(a_w[:, :, 0:2 * R2].rearrange("p k (m r) -> p k m r", r=RANK),
                     a_in[:, :, :, :].rearrange("p m k r -> p k m r")).then_inc(ah_ready, 1)
                for u in range(RING):
                    if u == 0:
                        act.wait_ge(b_loaded, 16 * COPIES * PAIR * (len(SEGS) * blk + 1))
                    finish_x1(blk, S0 // RING - 1, u)
                    split_gu(blk, 0, 0, u)
                form_t(blk, 0, ta_ps, 2 * R2, [(t_gate, 0), (t_up, R2)])

                for seg, n in enumerate(SEGS):
                    def finish_act(it, u):
                        if u % 2 != (not is_half(seg, it, u)):
                            return
                        f, par = 2 * it + u // 2, u // 2
                        if is_half(seg, it, u):
                            act.wait_ge(chunk_used[u], turn(blk, GU_AT[seg], it) + 1)
                            nc.scalar.activation(work[HALF:P, 0, :], gate_ps[par][0:HALF, :], ACT.Silu
                                                 ).then_inc(silu_ready, 1)
                            act.wait_ge(gu_read[par], (FT // 2) * blk + SEG_AT[seg] // 2 + it + 1)
                            copy(acth[0:HALF, f, :], work[0:HALF, 1, :]).then_inc(acth_ready, 1)
                            return
                        act.wait_ge(chunk_used[u], turn(blk, GU_AT[seg], it) + 1)
                        nc.scalar.activation(work[:, 0, :], gate_ps[par][:, :], ACT.Silu).then_inc(silu_ready, 1)
                        met()
                        act.wait_ge(gu_read[par], (FT // 2) * blk + SEG_AT[seg] // 2 + it + 1)
                        copy(row(acth, f), work[:, 1, :]).then_inc(acth_ready, 1)
                        if seg == X_SEG:
                            with act.If(blk < BLOCKS - 1):
                                met()
                                split_next_x(blk, f)

                    turns = 2 * n // RING - 1 - (seg == len(SEGS) - 1)
                    with act.Fori(0, turns) as it:
                        for u in range(RING):
                            finish_act(it, u)
                            split_gu(blk, seg, it + 1, u)
                    for it in range(turns, 2 * n // RING - 1):
                        for u in range(RING):
                            finish_act(it, u)
                            split_gu(blk, seg, it + 1, u)
                    act.wait_ge(ad_loaded, 16 * PAIR * (len(SEGS) * blk + seg + 1))
                    copy(ad_w[:, 0:n, 0:R2].rearrange("p k (b r) -> p k b r", r=RANK),
                         ad_in[:, :, 0:n, :].rearrange("p b k r -> p k b r")).then_inc(adh_ready, 1)
                    if seg == len(SEGS) - 1:
                        act.wait_ge(bd_loaded, 16 * COPIES * PAIR * (blk + 1))
                    for u in range(RING):
                        finish_act(2 * n // RING - 1, u)
                        if is_half(seg, 2 * n // RING - 1, u) and u % 2 == 0:
                            form_t(blk, 1, td_ps, R2, [(t_down, 0)])
                        split_down(blk, seg, 0, u)

                    if seg < len(SEGS) - 1:
                        for u in range(RING):
                            split_down(blk, seg, 1, u)
                        act.wait_ge(b_loaded, 16 * COPIES * PAIR * (len(SEGS) * blk + seg + 2))
                        for u in range(RING):
                            split_gu(blk, seg + 1, 0, u)
                    else:

                        def store(h):
                            par = h % 2
                            act.wait_ge(down_read[par], (3 * HT // 2) * blk + HT + h // 2 + 1)
                            act.dma_start(out[ds(HT * blk + h, 1), :, :].rearrange("a p n -> p (a n)"),
                                          stage[:, par, :]).then_inc(out_stored[par], 16)

                        more = blk < BLOCKS - 1
                        for u in range(RING):
                            split_down(blk, seg, 1, u)
                            store(u)
                        for u in range(RING):
                            with act.If(more):
                                after = next_block(blk)
                                if u == 0:
                                    form_sign(after, 0, 0)
                                form_sign(after, *divmod(u + 1, RING))
                                split_stage0(after, 0, u)
                            store(RING + u)
            for par in range(2):
                act.wait_ge(out_stored[par], 16 * (HT // 2) * BLOCKS)

        @block.vector
        def _(dve):
            def sub(o, a, b):
                return nc.vector.tensor_tensor(o, a, b, ALU.subtract)

            def add(o, a, b):
                return nc.vector.tensor_tensor(o, a, b, ALU.add)

            def split_next_x(blk, k):
                dve.wait_ge(xh_ready, HT * (blk + 1) + k + 1)
                sub(row(xl, k), x_in[:, :], row(xh, k)).then_inc(xl_ready, 1)

            def form_matrix(blk, it, u):
                o, par = 2 * it + u // 2, u // 2
                n = (HT // 2) * blk + it
                if u % 2 == 0:
                    dve.wait_ge(w_loaded[par], 16 * (n + 1))
                    tile = w_in[:, par, ds(o * P, P)]
                    add(tile, tile, ident_sb[:, :]).then_inc(w_ident[par], 1)
                    dve.wait_ge(w_ident[par], n + 1)
                dve.wait_ge(sign_ready[u], n + 1)
                add(raw[:, u, :], raw[:, u, :], w_in[:, par, :]).then_inc(wc_ready[u], 1)

            def split_stage0(blk, it, u):
                dve.wait_ge(hi_ready[u], turn(blk, 0, it) + 1)
                sub(lo[:, u, :], raw[:, u, :], hi[:, u, :]).then_inc(lo_ready[u], 1)

            def split_gu(blk, seg, it, u):
                f = 2 * it + u // 2
                dve.wait_ge(hi_ready[u], turn(blk, GU_AT[seg], it) + 1)
                q = slice(R2, 2 * R2)
                sub(b_w[q, u, :], b_in[q, u % 2, ds(f * P, P)], b_w[q, u, :])
                if is_half(seg, it, u):
                    sub(half_of(lo, u), raw[:, u, 0:H // 2].rearrange("p (k c) -> p k c", c=HALF), half_of(hi, u)
                        ).then_inc(lo_ready[u], 1)
                else:
                    sub(lo[:, u, :], raw[:, u, :], hi[:, u, :]).then_inc(lo_ready[u], 1)

            def split_down(blk, seg, it, u):
                n = SEGS[seg] * P
                dve.wait_ge(hi_ready[u], turn(blk, DN_AT[seg], it) + 1)
                if seg == len(SEGS) - 1:
                    h = 4 * it + u
                    q = slice(R2, 2 * R2)
                    sub(b_w[q, u, :], bd_in[q, ds(h * P, P)], b_w[q, u, :])
                sub(lo[:, u, 0:n], raw[:, u, 0:n], hi[:, u, 0:n]).then_inc(lo_ready[u], 1)

            def finish_x1(blk, it, u):
                if u % 2 == 0:
                    return
                o, par = 2 * it + u // 2, u // 2
                dve.wait_ge(x1h_ready[par], (HT // 2) * blk + it + 1)
                sub(row(x1l, o), row(x1, o), row(x1h, o)).then_inc(x1l_ready, 1)

            def form_t(blk, which, src, rows, parts):
                n = 2 * blk + which + 1
                dve.wait_ge(t_low, n)
                t = stage[0:rows, 1, :]
                add(t, src[0:rows, :], stage[0:rows, 0, :]).then_inc(t_sum, 1)
                dve.wait_ge(t_sum, n)
                nc.vector.tensor_tensor(t, t, own_sb[0:rows, :], ALU.mult).then_inc(t_own, 1)
                dve.wait_ge(t_own, n)
                for i, (dst, r) in enumerate(parts):
                    m = 3 * blk + 2 * which + i + 1
                    nc.vector.tensor_copy(dst[0:R2, :], stage[r:r + R2, 1, :]).then_inc(t_top, 1)
                    dve.wait_ge(t_top, m) if r == 0 else dve.wait_ge(t_hi, m)
                    sub(dst[2 * R2:3 * R2, :], stage[r:r + R2, 1, :], dst[r:r + R2, :]).then_inc(t_ready, 1)

            dve.wait_ge(consts_in, 16 * 3)
            nc.vector.tensor_scalar(coeff2[:, :], coeff_sb[:, :], 2.0, None, ALU.mult)
            nc.vector.tensor_scalar(ncoeff[:, :], coeff_sb[:, :], -1.0, None, ALU.mult).then_inc(coeffs_ready, 1)
            form_matrix(0, 0, 0)
            for k in range(HT):
                dve.wait_ge(xh_ready, k + 1)
                sub(xl[:, k, :], x1[:, k, :], xh[:, k, :]).then_inc(xl_ready, 1)
                if k == HT // 2 - 1:
                    split_stage0(0, 0, 0)
            form_matrix(0, 0, 1)
            for u in range(1, RING):
                form_matrix(0, *divmod(u + 1, RING))
                split_stage0(0, 0, u)
            dve.wait_ge(own_in, 16)

            with dve.Fori(0, BLOCKS) as blk:
                def stage0_step(it, u):
                    finish_x1(blk, it, u)
                    form_matrix(blk, it + 1 + (u + 1) // RING, (u + 1) % RING)
                    split_stage0(blk, it + 1, u)

                with dve.Fori(0, S0 // RING - 2) as it:
                    for u in range(RING):
                        stage0_step(it, u)
                it = S0 // RING - 2
                for u in range(RING - 1):
                    stage0_step(it, u)
                finish_x1(blk, it, RING - 1)
                split_stage0(blk, it + 1, RING - 1)
                dve.wait_ge(ah_ready, blk + 1)
                sub(a_w[:, :, 2 * R2:4 * R2].rearrange("p k (m r) -> p k m r", r=RANK),
                    a_in[:, :, :, :].rearrange("p m k r -> p k m r"),
                    a_w[:, :, 0:2 * R2].rearrange("p k (m r) -> p k m r", r=RANK)).then_inc(al_ready, 1)
                for u in range(RING):
                    finish_x1(blk, S0 // RING - 1, u)
                    split_gu(blk, 0, 0, u)
                form_t(blk, 0, ta_ps, 2 * R2, [(t_gate, 0), (t_up, R2)])

                for seg, n in enumerate(SEGS):
                    def finish_act(it, u):
                        if u % 2 != (not is_half(seg, it, u)):
                            return
                        f, par = 2 * it + u // 2, u // 2
                        done = FT * blk + SEG_AT[seg] + f + 1
                        dve.wait_ge(act_ready, done - 1)
                        dve.wait_ge(silu_ready, done)
                        if is_half(seg, it, u):
                            nc.vector.tensor_tensor(work[0:HALF, 1, :], work[HALF:P, 0, :], gate_ps[par][HALF:P, :],
                                                    ALU.mult).then_inc(gu_read[par], 1)
                            dve.wait_ge(acth_ready, done)
                            sub(acth[HALF:P, f, :], work[0:HALF, 1, :], acth[0:HALF, f, :]).then_inc(act_ready, 1)
                            return
                        nc.vector.tensor_tensor(work[:, 1, :], work[:, 0, :], up_ps[par][:, :], ALU.mult
                                                ).then_inc(gu_read[par], 1)
                        dve.wait_ge(acth_ready, done)
                        sub(row(actl, f), work[:, 1, :], row(acth, f)).then_inc(act_ready, 1)
                        if seg == X_SEG:
                            with dve.If(blk < BLOCKS - 1):
                                split_next_x(blk, f)

                    turns = 2 * n // RING - 1 - (seg == len(SEGS) - 1)
                    with dve.Fori(0, turns) as it:
                        for u in range(RING):
                            finish_act(it, u)
                            split_gu(blk, seg, it + 1, u)
                    for it in range(turns, 2 * n // RING - 1):
                        for u in range(RING):
                            finish_act(it, u)
                            split_gu(blk, seg, it + 1, u)
                    dve.wait_ge(adh_ready, len(SEGS) * blk + seg + 1)
                    sub(ad_w[:, 0:n, R2:2 * R2].rearrange("p k (b r) -> p k b r", r=RANK),
                        ad_in[:, :, 0:n, :].rearrange("p b k r -> p k b r"),
                        ad_w[:, 0:n, 0:R2].rearrange("p k (b r) -> p k b r", r=RANK)).then_inc(adl_ready, 1)
                    for u in range(RING):
                        finish_act(2 * n // RING - 1, u)
                        if is_half(seg, 2 * n // RING - 1, u) and u % 2 == 0:
                            form_t(blk, 1, td_ps, R2, [(t_down, 0)])
                        split_down(blk, seg, 0, u)

                    def finish_down(h):
                        par = h % 2
                        dve.wait_ge(chunk_used[h % RING], turn(blk, DN_AT[seg], h // RING) + 1)
                        if seg:
                            dve.wait_ge(down_read[par], (3 * HT // 2) * blk + (HT // 2) * (seg - 1) + h // 2 + 1)
                        if seg < len(SEGS) - 1:
                            dst = x1[:, h, :]
                        else:
                            dve.wait_ge(out_stored[par], 16 * ((HT // 2) * blk + h // 2))
                            dst = stage[:, par, :]
                        add(dst, x1[:, h, :], down_ps[par][:, :]).then_inc(down_read[par], 1)

                    if seg < len(SEGS) - 1:
                        for u in range(RING):
                            finish_down(u)
                            split_down(blk, seg, 1, u)
                        for u in range(RING):
                            finish_down(RING + u)
                            split_gu(blk, seg + 1, 0, u)
                    else:
                        more = blk < BLOCKS - 1
                        for u in range(RING):
                            finish_down(u)
                            split_down(blk, seg, 1, u)
                        for u in range(RING):
                            finish_down(RING + u)
                            with dve.If(more):
                                if u == 0:
                                    form_matrix(blk + 1, 0, 0)
                                form_matrix(blk + 1, *divmod(u + 1, RING))
                                split_stage0(blk + 1, 0, u)

        @block.tensor
        def _(pe):
            mm = nc.tensor.matmul

            def three(dst, u, k, vh, vl, first, last, lora=None):
                w = slice(k * P, (k + 1) * P)
                mm(dst, hi[:, u, w], vh, start=first, stop=False)
                if vl is not None:
                    mm(dst, hi[:, u, w], vl, start=False, stop=False)
                if last and lora is not None:
                    mm(dst, b_w[:, u, :], lora[:, :], start=False, stop=False)
                end = mm(dst, lo[:, u, w], vh, start=False, stop=last)
                if last:
                    end.then_inc(chunk_used[u], 1)

            with pe.Fori(0, BLOCKS) as blk:
                with pe.Fori(0, S0 // RING) as it:
                    for u in range(RING):
                        b, par = u % 2, u // 2
                        if b == 0:
                            pe.wait_ge(x1h_ready[par], (HT // 2) * blk + it)
                        pe.wait_ge(lo_ready[u], turn(blk, 0, it) + 1)
                        cols = slice(b * S, (b + 1) * S)
                        for k in range(HT):
                            if u == 0 and k % (HT // 2) == 0:
                                pe.wait_ge(xl_ready, HT * blk + k + HT // 2)
                            three(gate_ps[par][:, cols], u, k, xh[:, k, cols], xl[:, k, cols], k == 0, k == HT - 1)

                pe.wait_ge(al_ready, blk + 1)
                for k in range(HT):
                    if k == 0 or k == HT - 1:
                        pe.wait_ge(x1l_ready, HT * blk + (HT if k else HT - 1))
                    mm(ta_ps[:, :], a_w[:, k, :], x1h[:, k, :], start=k == 0, stop=False)
                    end = mm(ta_ps[:, :], a_w[:, k, :], x1l[:, k, :], start=False, stop=k == HT - 1)
                end.then_inc(t_done, 1)

                for seg, n in enumerate(SEGS):
                    def gate_or_up(it, u):
                        par = u // 2
                        if u % 2 == 0:
                            pe.wait_ge(gu_read[par], (FT // 2) * blk + SEG_AT[seg] // 2 + it)
                        pe.wait_ge(lo_ready[u], turn(blk, GU_AT[seg], it) + 1)
                        dst, t = ((gate_ps[par], t_gate), (up_ps[par], t_up))[u % 2]
                        for k in range(HT):
                            if k == HT - 1 and seg == 0:
                                pe.wait_ge(t_hi, 3 * blk + u % 2 + 1)
                                pe.wait_ge(t_ready, 3 * blk + u % 2 + 1)
                            three(dst[:, :], u, k, x1h[:, k, :], x1l[:, k, :], k == 0, k == HT - 1, t)

                    def gate_and_up(it, u):
                        par, dst = u // 2, gate_ps[u // 2][:, :]
                        pe.wait_ge(gu_read[par], (FT // 2) * blk + SEG_AT[seg] // 2 + it)
                        for v in (u, u + 1):
                            pe.wait_ge(lo_ready[v], turn(blk, GU_AT[seg], it) + 1)
                        for k in range(HT):
                            w = slice(k * P, (k + 1) * P)
                            mm(dst, hi[:, u, w], x1h[:, k, :], start=k == 0, stop=False)
                            mm(dst, hi[:, u, w], x1l[:, k, :], start=False, stop=False)
                            if k < HT - 1:
                                mm(dst, lo[:, u, w], x1h[:, k, :], start=False, stop=False)
                        mm(dst, b_w[:, u, :], t_gate[:, :], start=False, stop=False)
                        mm(dst, b_w[:, u + 1, :], t_up[:, :], start=False, stop=False)
                        for b, v in enumerate((u + 1, u)):
                            q = slice(b * S, (b + 1) * S)
                            mm(dst[:, q], lo[:, u, w], x1h[:, HT - 1, q], start=False, stop=b == 1
                               ).then_inc(chunk_used[v], 1)

                    with pe.Fori(0, 2 * n // RING - (seg == len(SEGS) - 1)) as it:
                        for u in range(RING):
                            gate_or_up(it, u)
                    if seg == len(SEGS) - 1:
                        it = 2 * n // RING - 1
                        gate_or_up(it, 0)
                        gate_or_up(it, 1)
                        gate_and_up(it, 2)

                    pe.wait_ge(adl_ready, len(SEGS) * blk + seg + 1)
                    for k in range(n):
                        if k == 0 or k == n - 1:
                            pe.wait_ge(act_ready, FT * blk + SEG_AT[seg] + (n if k else n - 1))
                        start, stop = seg == 0 and k == 0, seg == len(SEGS) - 1 and k == n - 1
                        end = mm(td_ps[0:2 * R2, :], ad_w[:, k, :], acth[:, k, :], start=start, stop=stop)
                        if not stop:
                            end = mm(td_ps[0:2 * R2, :], ad_w[:, k, :], actl[:, k, :], start=False, stop=False)
                    if seg == len(SEGS) - 1:
                        end.then_inc(t_done, 1)
                    with pe.Fori(0, HT // RING) as it:
                        for u in range(RING):
                            par = u % 2
                            pe.wait_ge(down_read[par], (3 * HT // 2) * blk + (HT // 2) * seg + 2 * it + u // 2)
                            pe.wait_ge(lo_ready[u], turn(blk, DN_AT[seg], it) + 1)
                            for k in range(n):
                                lora = t_down if seg == len(SEGS) - 1 else None
                                if lora is not None and k == n - 1:
                                    pe.wait_ge(t_hi, 3 * blk + 3)
                                    pe.wait_ge(t_ready, 3 * blk + 3)
                                three(down_ps[par][:, :], u, k, acth[:, k, :],
                                      None if SEG_AT[seg] + k == FT - 1 else actl[:, k, :], k == 0, k == n - 1, lora)


def kernel(x, condB_coeff, itok_B_2_6, mask_Bx4096x4096_ik1, L0_cond_W, L0_cond_b, L1_cond_W_gate, L1_cond_W_up,
           L1_cond_W_down, L1_cond_A_gate, L1_cond_B_gate, L1_cond_A_up, L1_cond_B_up, L1_cond_A_down,
           L1_cond_B_down):
    import concourse.bacc as bacc
    from concourse.bass_utils import run_bass_kernel_spmd

    FP = FT * P

    def pad_f(a, axis, before=0):
        zeros = np.zeros_like(np.take(a, range(HALF), axis))
        full, half = np.split(a, [F - HALF], axis)
        return np.concatenate([full, zeros, half] if before else [full, half, zeros], axis)

    def twice(a, axis):
        return np.concatenate([a, np.split(a, [F - HALF], axis)[1]], axis)

    def tiles(w, n_out, n_in):
        return w.reshape(n_out, P, n_in, P).transpose(0, 3, 2, 1).reshape(n_out, P, n_in * P)

    x, mask = np.asarray(x), np.asarray(mask_Bx4096x4096_ik1)
    wg, wu = (tiles(pad_f(np.asarray(w), 0), FT, HT) for w in (L1_cond_W_gate, L1_cond_W_up))
    for w in (wg, wu):
        w[-1, :, :H // 2] = w[-1].reshape(P, HT, P)[:, :, :HALF].reshape(P, H // 2)
    a_gate, a_up = (np.asarray(a)[0].reshape(ADAPTERS, RANK, HT, P).transpose(0, 3, 2, 1).reshape(ADAPTERS, P, -1)
                    for a in (L1_cond_A_gate, L1_cond_A_up))
    a_down = twice(np.asarray(L1_cond_A_down)[0], 2)
    a_down = a_down.reshape(ADAPTERS, RANK, FT, P).transpose(0, 3, 2, 1).reshape(ADAPTERS, P, -1)
    b_gate, b_up = (pad_f(np.asarray(b)[0].transpose(0, 2, 1), 2, before)
                    for b, before in ((L1_cond_B_gate, False), (L1_cond_B_up, True)))
    rows, cols = np.arange(2 * R2) % R2 // RANK, np.arange(T) // S
    arrays = {
        "x": x.reshape(BLOCKS, T, HT, P).transpose(0, 2, 3, 1).reshape(BLOCKS * HT, P, T),
        "mask": mask.reshape(BLOCKS, PAIR, HT, P, HT, P).transpose(0, 4, 1, 3, 2, 5).reshape(BLOCKS * S0, P, H),
        "coeff": np.broadcast_to(np.asarray(condB_coeff), (P, B)),
        "w0": tiles(np.asarray(L0_cond_W), HT, HT),
        "bias": np.asarray(L0_cond_b).reshape(HT, P).T,
        "wgu": np.stack([wg, wu], 1).reshape(2 * FT, P, H),
        "wd": tiles(twice(np.asarray(L1_cond_W_down), 1), HT, FT),
        "a_gate": a_gate, "a_up": a_up, "a_down": a_down,
        "b_gu": np.stack([b_gate, b_up], 2),
        "b_down": np.asarray(L1_cond_B_down)[0].transpose(0, 2, 1),
        "idx": np.asarray(itok_B_2_6).reshape(1, B),
        "ident": np.eye(P, dtype=np.float32),
        "own": np.where(rows[:, None] == cols[None, :], np.float32(LORA_SCALE), np.float32(0)),
    }
    arrays = {f"in_{k}": np.ascontiguousarray(v) for k, v in arrays.items()}
    nc = bacc.Bacc("TRN2", target_bir_lowering=False, num_devices=1)
    args = [nc.dram_tensor(k, v.shape, mybir.dt.from_np(v.dtype), kind="ExternalInput").ap() for k, v in arrays.items()]
    args.append(nc.dram_tensor("out", (BLOCKS * HT, P, T), mybir.dt.float32, kind="ExternalOutput").ap())
    build(nc, *args)
    got = run_bass_kernel_spmd(nc, [arrays], core_ids=[0]).results[0]["out"]
    return got.reshape(BLOCKS, H, T).transpose(0, 2, 1).reshape(B, S, H)
```

```python
from contextlib import ExitStack

import numpy as np

import concourse.bass as bass
from concourse import mybir

P = 128
B, S, H, F, ADAPTERS, RANK = 8, 256, 1024, 2752, 16, 16
LORA_SCALE = 0.5
BLOCKS, PAIR = 4, 2
T = PAIR * S
HT = H // P
FT = -(-F // P)
HALF = F % P
assert 2 * HALF == P
SEGS = [8, 8, 6]
SEG_AT = [0, 8, 16]
X_SEG = 1
RING = 4
S0 = HT * PAIR
GU_AT, DN_AT, _at = [], [], S0
for _n in SEGS:
    GU_AT.append(_at)
    DN_AT.append(_at + 2 * _n)
    _at += 2 * _n + HT
CHUNKS = _at
MIX_AT = DN_AT[-1]
MIX = [(o, b) for o in range(HT) for b in range(PAIR + 1)]
MIX_LOOPS = 2
MIX_TURN = len(MIX) // MIX_LOOPS
AHEAD = RING
assert HT == SEGS[0] and MIX_TURN % RING == 0 and MIX_AT % RING == 0
TURNS = CHUNKS // RING
R2 = PAIR * RANK
COPIES = 3
TR = COPIES * R2
DR = 2 * RANK
assert H == max(SEGS) * P and TR + DR == P and HALF + 2 * DR == P


def build(nc, x, mask, coeff, w0, bias, wgu, wd, a_gate, a_up, a_down, b_gu, b_down, idx, ident, own,
          pick_rows, out):
    f32, f32r, i32 = mybir.dt.float32, mybir.dt.float32r, mybir.dt.int32
    ACT, ALU = mybir.ActivationFunctionType, mybir.AluOpType
    ds = bass.ds

    def row(t, i):
        if isinstance(i, int):
            return t[:, i, :]
        return t[:, ds(i, 1), :].rearrange("p a n -> p (a n)")

    def next_block(blk):
        return nc.s_assert_within(blk + 1, 1, BLOCKS - 1, skip_runtime_bounds_check_because=
                                  "the branch is taken before the last block only")

    def is_half(seg, it, u):
        return seg == len(SEGS) - 1 and isinstance(it, int) and 2 * it + u // 2 == SEGS[seg] - 1

    def half_of(t, u):
        c = (u % 2) * HALF
        return t[:, u - u % 2, :].rearrange("p (k c) -> p k c", c=P)[:, :, c:c + HALF]

    def turn(blk, at, it):
        return TURNS * blk + at // RING + it

    def mixed(blk, p, loop=0):
        return p % RING, turn(blk, MIX_AT, p // RING) + MIX_TURN // RING * loop

    with ExitStack() as ctx:
        def sb(name, shape, dt):
            return ctx.enter_context(nc.sbuf_tensor(name, shape, dt))

        def ps(name):
            return ctx.enter_context(nc.psum_tensor(name, [P, T], f32))

        def sem(name):
            return ctx.enter_context(nc.semaphore(name))

        def sems(name, n):
            return [sem(f"{name}{i}") for i in range(n)]

        raw = sb("raw", [P, RING, H], f32)
        raw_i = raw[:, :, :].bitcast(i32)
        hi = sb("hi", [P, RING, H], f32r)
        lo = sb("lo", [P, RING, H], f32r)
        w_in = sb("w_in", [P, 2, H], f32)
        xh = sb("xh", [P, HT, T], f32r)
        xl = sb("xl", [P, HT, T], f32r)
        x1 = sb("x1", [P, HT, T], f32)
        x1h = sb("x1h", [P, HT, T], f32r)
        x1l = sb("x1l", [P, HT, T], f32r)
        acth = sb("acth", [P, max(SEGS), T], f32r)
        actl = sb("actl", [P, max(SEGS), T], f32r)
        x_in = sb("x_in", [P, T], f32)
        work = sb("work", [P, 2, T], f32)
        stage = sb("stage", [P, 2, T], f32)
        b_in = sb("b_in", [P, 2, max(SEGS) * P], f32)
        bd_in = b_in[TR:P, :, :]
        b_w = sb("b_w", [P, RING, P], f32r)
        a_in = sb("a_in", [P, 2 * PAIR, HT, RANK], f32)
        a_w = sb("a_w", [P, HT, 4 * R2], f32r)
        ad_in = sb("ad_in", [P, PAIR, max(SEGS), RANK], f32)
        ad_w = sb("ad_w", [P, max(SEGS), PAIR * 2 * DR], f32r)
        t_gate = sb("t_gate", [TR, T], f32r)
        t_up = sb("t_up", [TR, T], f32r)
        act_t = sb("act_t", [P, T], f32r)
        pick = sb("pick", [DR, 2], f32)
        own_sb = sb("own_sb", [2 * R2, T], f32)
        ident_sb = sb("ident_sb", [P, P], f32)
        bias_sb = sb("bias_sb", [P, HT], f32)
        coeff_sb = sb("coeff_sb", [P, B], f32)
        coeff2 = sb("coeff2", [P, B], f32)
        ncoeff = sb("ncoeff", [P, B], f32)
        silu_warm = sb("silu_warm", [P, 1], f32)
        idx_sb = sb("idx_sb", [1, B], i32)

        gate_ps = [ps("gate_ps0"), ps("gate_ps1")]
        up_ps = [ps("up_ps0"), ps("up_ps1")]
        down_ps = [ps("down_ps0"), ps("down_ps1")]
        ta_ps = ps("ta_ps")
        td_ps = ps("td_ps")

        coeff_in = sem("coeff_in")
        ident_in = sem("ident_in")
        late_in = sem("late_in")
        idx_in = sem("idx_in")
        coeffs_ready = sem("coeffs_ready")
        x0_loaded = sems("x0_loaded", HT)
        x_loaded = sem("x_loaded")
        xh_ready = sem("xh_ready")
        xl_ready = sem("xl_ready")
        w_loaded = sems("w_loaded", 2)
        w_ident = sems("w_ident", 2)
        sign_ready = sems("sign_ready", 2 * PAIR)
        wc_ready = sems("wc_ready", 2 * PAIR)
        raw_loaded = sems("raw_loaded", RING)
        hi_ready = sems("hi_ready", RING)
        lo_ready = sems("lo_ready", RING)
        chunk_used = sems("chunk_used", RING)
        x1h_ready = sems("x1h_ready", 2)
        x1l_ready = sems("x1l_ready", 2)
        x1_ready = sem("x1_ready")
        a_loaded = sem("a_loaded")
        ah_ready = sem("ah_ready")
        al_ready = sem("al_ready")
        ad_loaded = sem("ad_loaded")
        adh_ready = sem("adh_ready")
        adl_ready = sem("adl_ready")
        b_loaded = sem("b_loaded")
        bd_loaded = sem("bd_loaded")
        t_done = sem("t_done")
        t_low = sem("t_low")
        t_sum = sem("t_sum")
        t_own = sem("t_own")
        t_hi = sem("t_hi")
        t_top = sem("t_top")
        t_ready = sem("t_ready")
        td_low = sem("td_low")
        td_sum = sem("td_sum")
        td_hi = sem("td_hi")
        td_picked = sem("td_picked")
        td_ready = sem("td_ready")
        act_t_ready = sem("act_t_ready")
        silu_ready = sem("silu_ready")
        gu_read = sems("gu_read", 2)
        acth_ready = sem("acth_ready")
        act_ready = sem("act_ready")
        down_read = sems("down_read", 2)
        out_stored = sems("out_stored", 2)

        def ad_rows(n, q):
            cols = ad_w[:, 0:n, :].rearrange("p k (b q r) -> p k b q r", q=4, r=RANK)
            return cols[:, :, :, q:q + 1, :].rearrange("p k b q r -> p k b (q r)")

        block = ctx.enter_context(nc.Block())

        @block.sync
        def _(sp):
            def met():
                sp.wait_ge(coeff_in, 16)

            def load_chunk(slot, turns, src):
                met()
                sp.wait_ge(lo_ready[slot], turns)
                sp.dma_start(raw[:, slot, 0:src.shape[-1]], src).then_inc(raw_loaded[slot], 16)

            def w_dma(it, par):
                sp.dma_start(w_in[:, par, :], w0[ds(2 * it + par, 1), :, :].rearrange("a p n -> p (a n)")
                             ).then_inc(w_loaded[par], 16)

            def mask_dma(blk, it, u, slot):
                sp.dma_start(raw_i[:, slot, :],
                             mask[ds(S0 * blk + 4 * it + u, 1), :, :].rearrange("a p n -> p (a n)")
                             ).then_inc(raw_loaded[slot], 16)

            def load_w(blk, it, par):
                met()
                sp.wait_ge(wc_ready[PAIR * par + 1], (HT // 2) * blk + it)
                w_dma(it, par)

            def load_mask(blk, it, u, slot, turns):
                met()
                sp.wait_ge(lo_ready[slot], turns)
                mask_dma(blk, it, u, slot)

            def load_down(blk, seg, h, slot, turns):
                cols = slice(SEG_AT[seg] * P, (SEG_AT[seg] + SEGS[seg]) * P)
                load_chunk(slot, turns, wd[ds(h, 1), :, cols].rearrange("a p n -> p (a n)"))

            sp.dma_start(coeff_sb[:, :], coeff).then_inc(coeff_in, 16)
            mask_dma(0, 0, 0, 0)
            w_dma(0, 0)
            sp.dma_start(ident_sb[:, :], ident).then_inc(ident_in, 16)
            for k in range(HT):
                if k == HT // 2:
                    mask_dma(0, 0, 1, 1)
                sp.dma_start(x1[:, k, :], x[k, :, :]).then_inc(x0_loaded[k], 16)
            mask_dma(0, 0, 2, 2)
            w_dma(0, 1)
            mask_dma(0, 0, 3, 3)
            sp.dma_start(bias_sb[:, :], bias).then_inc(late_in, 16)
            sp.dma_start(own_sb[:, :], own).then_inc(late_in, 16)
            sp.dma_start(pick[:, :], pick_rows).then_inc(late_in, 16)
            with sp.Fori(1, S0 // RING) as it:
                for u in range(RING):
                    if u % 2 == 0:
                        load_w(0, it, u // 2)
                    load_mask(0, it, u, u, turn(0, 0, it))
            with sp.Fori(0, BLOCKS) as blk:
                for seg, n in enumerate(SEGS):
                    last = seg == len(SEGS) - 1
                    whole = 2 * n // RING - last
                    with sp.Fori(0, whole) as it:
                        for u in range(RING):
                            c = 2 * SEG_AT[seg] + 4 * it + u
                            load_chunk(u, turn(blk, GU_AT[seg], it), wgu[ds(c, 1), :, :].rearrange("a p n -> p (a n)"))
                    if last:
                        for u in range(RING):
                            c = 2 * SEG_AT[seg] + 4 * whole + u
                            load_chunk(u, turn(blk, GU_AT[seg], whole), wgu[c, :, :] if u < 2 else wgu[c, :, 0:H // 2])
                        with sp.If(blk < BLOCKS - 1):
                            after = next_block(blk)
                            with sp.Fori(0, MIX_LOOPS) as loop:
                                for p, (o, b) in enumerate(MIX[:MIX_TURN]):
                                    slot, turns = mixed(blk, p, loop)
                                    it, par = (HT // 4) * loop + o // 2, o % 2
                                    if b == PAIR:
                                        load_down(blk, seg, (HT // MIX_LOOPS) * loop + o, slot, turns)
                                    else:
                                        if b == 0:
                                            load_w(after, it, par)
                                        load_mask(after, it, PAIR * par + b, slot, turns)

                    def loads_down():
                        with sp.Fori(0, HT // RING) as it:
                            for u in range(RING):
                                load_down(blk, seg, 4 * it + u, u, turn(blk, DN_AT[seg], it))

                    if last:
                        with sp.If(blk >= BLOCKS - 1):
                            loads_down()
                    else:
                        loads_down()

        @block.gpsimd
        def _(pool):
            def load_a_down(seg, adapter):
                for b in range(PAIR):
                    src = a_down[ds(adapter[b], 1), :, SEG_AT[seg] * RANK:(SEG_AT[seg] + SEGS[seg]) * RANK]
                    pool.dma_start(ad_in[:, b, 0:SEGS[seg], :].rearrange("p k r -> p (k r)"),
                                 src.rearrange("a p n -> p (a n)")).then_inc(ad_loaded, 16)

            def load_b_gu(seg, adapter):
                lo_f, n = SEG_AT[seg] * P, SEGS[seg] * P
                for q in range(COPIES):
                    for b in range(PAIR):
                        r = q * R2 + b * RANK
                        pool.dma_start(b_in[r:r + RANK, :, 0:n],
                                     b_gu[ds(adapter[b], 1), :, :, lo_f:lo_f + n].rearrange("a r g n -> (a r) g n")
                                     ).then_inc(b_loaded, 16)

            def adapters(blk):
                return [pool.value_load(idx_sb[0:1, ds(PAIR * blk + b, 1)], min_val=0, max_val=ADAPTERS - 1)
                        for b in range(PAIR)]

            def load_first(adapter):
                for m, a in enumerate((a_gate, a_up)):
                    for b in range(PAIR):
                        pool.dma_start(a_in[:, PAIR * m + b, :, :].rearrange("p k r -> p (k r)"),
                                       a[ds(adapter[b], 1), :, :].rearrange("a p n -> p (a n)")).then_inc(a_loaded, 16)
                load_a_down(0, adapter)
                load_b_gu(0, adapter)

            pool.dma_start(idx_sb[:, :], idx).then_inc(idx_in, 16)
            pool.wait_ge(idx_in, 16)
            pool.wait_ge(lo_ready[RING - 1], 2)
            load_first(adapters(0))
            with pool.Fori(0, BLOCKS) as blk:
                adapter = adapters(blk)
                for seg in range(1, len(SEGS)):
                    pool.wait_ge(adl_ready, len(SEGS) * blk + seg)
                    pool.wait_ge(lo_ready[RING - 1], turn(blk, DN_AT[seg - 1], 0))
                    load_a_down(seg, adapter)
                    load_b_gu(seg, adapter)
                    if seg == X_SEG:
                        for q in range(2):
                            for b in range(PAIR):
                                pool.dma_start(bd_in[q * RANK:(q + 1) * RANK, b, :],
                                               b_down[ds(adapter[b], 1), :, :].rearrange("a r n -> (a r) n")
                                               ).then_inc(bd_loaded, 16)
                        with pool.If(blk < BLOCKS - 1):
                            after = next_block(blk)
                            with pool.Fori(0, HT) as k:
                                pool.wait_ge(xl_ready, HT * after + k)
                                pool.dma_start(x_in[:, :], x[ds(HT * after + k, 1), :, :].rearrange("a p n -> p (a n)")
                                               ).then_inc(x_loaded, 16)
                with pool.If(blk < BLOCKS - 1):
                    pool.wait_ge(adl_ready, len(SEGS) * (blk + 1))
                    pool.wait_ge(lo_ready[RING - 1], turn(blk, DN_AT[-1], 0))
                    load_first(adapters(next_block(blk)))

        @block.scalar
        def _(act):
            def copy(o, i):
                return nc.scalar.activation(o, i, ACT.Copy)

            def met():
                act.wait_ge(coeffs_ready, 1)

            def split_next_x(blk, k):
                act.wait_ge(x_loaded, 16 * (HT * blk + k + 1))
                copy(row(xh, k), x_in[:, :]).then_inc(xh_ready, 1)

            def form_sign(blk, it, u, slot, turns):
                b = PAIR * blk + u % 2
                count = act.snap(act.to_reg(16 * (turns + 1)))
                met()
                act.wait_ge(raw_loaded[slot], count)
                nc.scalar.activation(raw[:, slot, :], raw_i[:, slot, :], ACT.Identity, bias=ncoeff[:, ds(b, 1)],
                                     scale=coeff2[:, ds(b, 1)]).then_inc(sign_ready[u], 1)

            def split_matrix(blk, it, u, slot, turns):
                act.wait_ge(wc_ready[u], (HT // 2) * blk + it + 1)
                act.wait_ge(chunk_used[slot], turns)
                copy(hi[:, slot, :], raw[:, slot, :]).then_inc(hi_ready[slot], 1)

            def split_gu(blk, seg, it, u):
                f = 2 * it + u // 2
                met()
                act.wait_ge(chunk_used[u], turn(blk, GU_AT[seg], it))
                copy(b_w[0:TR, u, :], b_in[0:TR, u % 2, ds(f * P, P)])
                act.wait_ge(raw_loaded[u], 16 * (turn(blk, GU_AT[seg], it) + 1))
                if is_half(seg, it, u):
                    copy(half_of(hi, u), raw[:, u, 0:H // 2].rearrange("p (k c) -> p k c", c=HALF)
                         ).then_inc(hi_ready[u], 1)
                else:
                    copy(hi[:, u, :], raw[:, u, :]).then_inc(hi_ready[u], 1)

            def split_down(seg, h, slot, turns):
                n = SEGS[seg] * P
                met()
                act.wait_ge(chunk_used[slot], turns)
                if seg == len(SEGS) - 1:
                    copy(lo[TR:P, slot, n - P:n], bd_in[:, 0, ds(h * P, P)])
                    copy(b_w[TR:P, slot, :], bd_in[:, 1, ds(h * P, P)])
                act.wait_ge(raw_loaded[slot], 16 * (turns + 1))
                copy(hi[:, slot, 0:n], raw[:, slot, 0:n]).then_inc(hi_ready[slot], 1)

            def finish_x1(o, par, slot, turns):
                met()
                act.wait_ge(chunk_used[slot], turns + 1)
                nc.scalar.activation(row(x1h, o), gate_ps[par][:, :], ACT.Identity, bias=bias_sb[:, ds(o, 1)]
                                     ).then_inc(x1h_ready[par], 1)

            def form_t_gu(blk):
                act.wait_ge(t_done, 2 * blk + 1)
                copy(work[0:2 * R2, 0, :], ta_ps[2 * R2:4 * R2, :]).then_inc(t_low, 1)
                act.wait_ge(t_own, blk + 1)
                for dst, r in ((t_gate, 0), (t_up, R2)):
                    copy(dst[R2:2 * R2, :], work[r:r + R2, 1, :]).then_inc(t_hi, 1)

            def form_t_down(blk):
                copy(act_t[0:HALF, :], work[0:HALF, 1, :]).then_inc(act_t_ready, 1)
                act.wait_ge(t_done, 2 * blk + 2)
                for b in range(PAIR):
                    r, cols = 2 * DR * b, slice(b * S, (b + 1) * S)
                    nc.scalar.activation(work[r:r + DR, 0, cols], td_ps[r + DR:r + 2 * DR, cols], ACT.Copy,
                                         scale=LORA_SCALE).then_inc(td_low, 1)

            def split_t_down(blk):
                act.wait_ge(td_sum, PAIR * (blk + 1))
                copy(t_gate[0:DR, :], work[0:DR, 1, :]).then_inc(td_hi, 1)

            act.wait_ge(coeffs_ready, 1)
            nc.scalar.activation(silu_warm[:, :], coeff_sb[:, 0:1], ACT.Silu)
            form_sign(0, 0, 0, 0, 0)
            for k in range(HT):
                if k == HT // 2:
                    form_sign(0, 0, 1, 1, 0)
                act.wait_ge(x0_loaded[k], 16)
                copy(xh[:, k, :], x1[:, k, :]).then_inc(xh_ready, 1)
                if k == 0:
                    split_matrix(0, 0, 0, 0, 0)
                if k == HT // 2 + 1:
                    split_matrix(0, 0, 1, 1, 0)
            for u in (2, 3):
                form_sign(0, 0, u, u, 0)
            for u in (2, 3):
                split_matrix(0, 0, u, u, 0)
            form_sign(0, 1, 0, 0, 1)
            act.wait_ge(late_in, 16 * 3)

            def stage0_step(it, u):
                if u % 2:
                    finish_x1(2 * it + u // 2, u // 2, u, turn(0, 0, it))
                if not isinstance(it, int) or u < RING - 1:
                    v, then = (u + 1) % RING, it + 1 + (u + 1) // RING
                    form_sign(0, then, v, v, turn(0, 0, then))
                split_matrix(0, it + 1, u, u, turn(0, 0, it + 1))

            def split_a_gu(blk):
                act.wait_ge(a_loaded, 16 * 2 * PAIR * (blk + 1))
                copy(a_w[:, :, 0:2 * R2].rearrange("p k (m r) -> p k m r", r=RANK),
                     a_in[:, :, :, :].rearrange("p m k r -> p k m r")).then_inc(ah_ready, 1)
                act.wait_ge(b_loaded, 16 * COPIES * PAIR * (len(SEGS) * blk + 1))

            with act.Fori(0, S0 // RING - 2) as it:
                for u in range(RING):
                    stage0_step(it, u)
            for u in range(RING):
                stage0_step(S0 // RING - 2, u)
            split_a_gu(0)
            for u in range(RING):
                it = S0 // RING - 1
                if u % 2:
                    finish_x1(2 * it + u // 2, u // 2, u, turn(0, 0, it))
                split_gu(0, 0, 0, u)

            with act.Fori(0, BLOCKS) as blk:
                form_t_gu(blk)

                for seg, n in enumerate(SEGS):
                    def finish_act(it, u):
                        if u % 2 != (not is_half(seg, it, u)):
                            return
                        f, par = 2 * it + u // 2, u // 2
                        if is_half(seg, it, u):
                            act.wait_ge(chunk_used[u], turn(blk, GU_AT[seg], it) + 1)
                            nc.scalar.activation(work[HALF:P, 0, :], gate_ps[par][0:HALF, :], ACT.Silu
                                                 ).then_inc(silu_ready, 1)
                            act.wait_ge(gu_read[par], (FT // 2) * blk + SEG_AT[seg] // 2 + it + 1)
                            copy(acth[0:HALF, f, :], work[0:HALF, 1, :]).then_inc(acth_ready, 1)
                            return
                        act.wait_ge(chunk_used[u], turn(blk, GU_AT[seg], it) + 1)
                        nc.scalar.activation(work[:, 0, :], gate_ps[par][:, :], ACT.Silu).then_inc(silu_ready, 1)
                        met()
                        act.wait_ge(gu_read[par], (FT // 2) * blk + SEG_AT[seg] // 2 + it + 1)
                        copy(row(acth, f), work[:, 1, :]).then_inc(acth_ready, 1)
                        if seg == X_SEG:
                            with act.If(blk < BLOCKS - 1):
                                met()
                                split_next_x(blk, f)

                    turns = 2 * n // RING - 1 - (seg == len(SEGS) - 1)
                    with act.Fori(0, turns) as it:
                        for u in range(RING):
                            finish_act(it, u)
                            split_gu(blk, seg, it + 1, u)
                    for it in range(turns, 2 * n // RING - 1):
                        for u in range(RING):
                            finish_act(it, u)
                            split_gu(blk, seg, it + 1, u)
                    act.wait_ge(ad_loaded, 16 * PAIR * (len(SEGS) * blk + seg + 1))
                    if seg == len(SEGS) - 1:
                        act.wait_ge(bd_loaded, 16 * 2 * PAIR * (blk + 1))
                    for q in range(2):
                        copy(ad_rows(n, q), ad_in[:, :, 0:n, :].rearrange("p b k r -> p k b r")).then_inc(adh_ready, 1)

                    def last_act(u):
                        finish_act(2 * n // RING - 1, u)

                    if seg < len(SEGS) - 1:
                        for u in range(RING):
                            last_act(u)
                            split_down(seg, u, u, turn(blk, DN_AT[seg], 0))
                        for u in range(RING):
                            split_down(seg, RING + u, u, turn(blk, DN_AT[seg], 1))
                        act.wait_ge(b_loaded, 16 * COPIES * PAIR * (len(SEGS) * blk + seg + 2))
                        for u in range(RING):
                            split_gu(blk, seg + 1, 0, u)
                        continue

                    def store(h):
                        par = h % 2
                        act.wait_ge(down_read[par], (3 * HT // 2) * blk + HT + h // 2 + 1)
                        act.dma_start(out[ds(HT * blk + h, 1), :, :].rearrange("a p n -> p (a n)"),
                                      stage[:, par, :]).then_inc(out_stored[par], 16)

                    with act.If(blk < BLOCKS - 1):
                        after = next_block(blk)

                        def sign(p):
                            o, b = MIX[p]
                            if b < PAIR:
                                form_sign(after, o // 2, PAIR * (o % 2) + b, *mixed(blk, p))

                        def split(p):
                            o, b = MIX[p]
                            if b < PAIR:
                                split_matrix(after, o // 2, PAIR * (o % 2) + b, *mixed(blk, p))
                            else:
                                split_down(seg, o, *mixed(blk, p))

                        def finish(p):
                            o, b = MIX[p]
                            if b == PAIR - 1:
                                finish_x1(o, o % 2, *mixed(blk, p))

                        def store_last(p):
                            o, b = MIX[p]
                            if b == 0 and o:
                                store(o - 1)

                        sign(0)
                        for p in range(AHEAD):
                            last_act(p)
                            if p == AHEAD - 1:
                                form_t_down(blk)
                            sign(p + 1)
                            split(p)
                        split_t_down(blk)
                        for p in range(AHEAD, len(MIX)):
                            finish(p - AHEAD)
                            if p + 1 < len(MIX):
                                sign(p + 1)
                            split(p)
                            store_last(p - AHEAD)
                        split_a_gu(after)
                        for u in range(RING):
                            finish(len(MIX) - AHEAD + u)
                            split_gu(after, 0, 0, u)
                            store_last(len(MIX) - AHEAD + u)
                        store(HT - 1)
                    with act.If(blk >= BLOCKS - 1):
                        for u in range(RING):
                            last_act(u)
                            if seg == len(SEGS) - 1 and u == RING // 2:
                                form_t_down(blk)
                                split_t_down(blk)
                            split_down(seg, u, u, turn(blk, DN_AT[seg], 0))
                        for u in range(RING):
                            split_down(seg, RING + u, u, turn(blk, DN_AT[seg], 1))
                            store(u)
                        for u in range(RING):
                            store(RING + u)
            for par in range(2):
                act.wait_ge(out_stored[par], 16 * (HT // 2) * BLOCKS)

        @block.vector
        def _(dve):
            def sub(o, a, b):
                return nc.vector.tensor_tensor(o, a, b, ALU.subtract)

            def add(o, a, b):
                return nc.vector.tensor_tensor(o, a, b, ALU.add)

            def split_next_x(blk, k):
                dve.wait_ge(xh_ready, HT * (blk + 1) + k + 1)
                sub(row(xl, k), x_in[:, :], row(xh, k)).then_inc(xl_ready, 1)

            def form_matrix(blk, it, u, slot):
                o, par = 2 * it + u // 2, u // 2
                n = (HT // 2) * blk + it
                if u % 2 == 0:
                    dve.wait_ge(w_loaded[par], 16 * (n + 1))
                    tile = w_in[:, par, ds(o * P, P)]
                    add(tile, tile, ident_sb[:, :]).then_inc(w_ident[par], 1)
                    dve.wait_ge(w_ident[par], n + 1)
                dve.wait_ge(sign_ready[u], n + 1)
                add(raw[:, slot, :], raw[:, slot, :], w_in[:, par, :]).then_inc(wc_ready[u], 1)

            def split_matrix(slot, turns):
                dve.wait_ge(hi_ready[slot], turns + 1)
                sub(lo[:, slot, :], raw[:, slot, :], hi[:, slot, :]).then_inc(lo_ready[slot], 1)

            def split_gu(blk, seg, it, u):
                f = 2 * it + u // 2
                dve.wait_ge(hi_ready[u], turn(blk, GU_AT[seg], it) + 1)
                q = slice(R2, 2 * R2)
                sub(b_w[q, u, :], b_in[q, u % 2, ds(f * P, P)], b_w[q, u, :])
                if is_half(seg, it, u):
                    sub(half_of(lo, u), raw[:, u, 0:H // 2].rearrange("p (k c) -> p k c", c=HALF), half_of(hi, u)
                        ).then_inc(lo_ready[u], 1)
                else:
                    sub(lo[:, u, :], raw[:, u, :], hi[:, u, :]).then_inc(lo_ready[u], 1)

            def split_down(seg, h, slot, turns):
                n = SEGS[seg] * P
                dve.wait_ge(hi_ready[slot], turns + 1)
                if seg == len(SEGS) - 1:
                    n -= P
                    for b, tile in ((0, lo[:, slot, n:n + P]), (1, b_w[:, slot, :])):
                        sub(tile[0:HALF, :], raw[0:HALF, slot, n:n + P], hi[0:HALF, slot, n:n + P])
                        sub(tile[HALF:TR, :], bd_in[:, b, ds(h * P, P)], tile[TR:P, :])
                sub(lo[:, slot, 0:n], raw[:, slot, 0:n], hi[:, slot, 0:n]).then_inc(lo_ready[slot], 1)

            def finish_x1(blk, o, par, half):
                dve.wait_ge(x1h_ready[par], (HT // 2) * blk + half + 1)
                nc.vector.scalar_tensor_tensor(out=row(x1l, o), in0=gate_ps[par][:, :], scalar=bias_sb[:, ds(o, 1)],
                                               in1=row(x1h, o), op0=ALU.add, op1=ALU.subtract
                                               ).then_inc(x1l_ready[par], 1)

            def form_t_gu(blk):
                dve.wait_ge(t_low, blk + 1)
                t = work[0:2 * R2, 1, :]
                add(t, ta_ps[0:2 * R2, :], work[0:2 * R2, 0, :]).then_inc(t_sum, 1)
                dve.wait_ge(t_sum, blk + 1)
                nc.vector.tensor_tensor(t, t, own_sb[:, :], ALU.mult).then_inc(t_own, 1)
                dve.wait_ge(t_own, blk + 1)
                for i, (dst, r) in enumerate(((t_gate, 0), (t_up, R2))):
                    m = 2 * blk + i + 1
                    nc.vector.tensor_copy(dst[0:R2, :], work[r:r + R2, 1, :]).then_inc(t_top, 1)
                    dve.wait_ge(t_top, m) if r == 0 else dve.wait_ge(t_hi, m)
                    sub(dst[2 * R2:3 * R2, :], work[r:r + R2, 1, :], dst[r:r + R2, :]).then_inc(t_ready, 1)

            def form_t_down(blk):
                dve.wait_ge(td_low, PAIR * (blk + 1))
                for b in range(PAIR):
                    r, cols = 2 * DR * b, slice(b * S, (b + 1) * S)
                    nc.vector.scalar_tensor_tensor(
                        out=work[0:DR, 1, cols], in0=td_ps[r:r + DR, cols], scalar=LORA_SCALE,
                        in1=work[r:r + DR, 0, cols], op0=ALU.mult, op1=ALU.add).then_inc(td_sum, 1)
                dve.wait_ge(td_sum, PAIR * (blk + 1))
                nc.vector.tensor_scalar(work[0:DR, 0, :], work[0:DR, 1, :], pick[:, 0:1], None, ALU.mult
                                        ).then_inc(td_picked, 1)

            def split_t_down(blk):
                dve.wait_ge(td_picked, blk + 1)
                dve.wait_ge(td_hi, blk + 1)
                for r in (HALF, HALF + DR):
                    nc.vector.scalar_tensor_tensor(
                        out=act_t[r:r + DR, :], in0=t_gate[0:DR, :], scalar=pick[:, 1:2],
                        in1=work[0:DR, 0, :], op0=ALU.mult, op1=ALU.add).then_inc(td_ready, 1)

            dve.wait_ge(coeff_in, 16)
            nc.vector.tensor_scalar(coeff2[:, :], coeff_sb[:, :], 2.0, None, ALU.mult)
            nc.vector.tensor_scalar(ncoeff[:, :], coeff_sb[:, :], -1.0, None, ALU.mult).then_inc(coeffs_ready, 1)
            dve.wait_ge(ident_in, 16)
            form_matrix(0, 0, 0, 0)
            for k in range(HT):
                if k == HT // 2:
                    form_matrix(0, 0, 1, 1)
                dve.wait_ge(xh_ready, k + 1)
                sub(xl[:, k, :], x1[:, k, :], xh[:, k, :]).then_inc(xl_ready, 1)
                if k == 0:
                    split_matrix(0, 0)
                if k == HT // 2 + 1:
                    split_matrix(1, 0)
            for u in (2, 3):
                form_matrix(0, 0, u, u)
            for u in (2, 3):
                split_matrix(u, 0)
            form_matrix(0, 1, 0, 0)
            dve.wait_ge(late_in, 16 * 3)

            def stage0_step(it, u):
                if u % 2:
                    finish_x1(0, 2 * it + u // 2, u // 2, it)
                if not isinstance(it, int) or u < RING - 1:
                    form_matrix(0, it + 1 + (u + 1) // RING, (u + 1) % RING, (u + 1) % RING)
                split_matrix(u, turn(0, 0, it + 1))

            def split_a_gu(blk):
                dve.wait_ge(ah_ready, blk + 1)
                sub(a_w[:, :, 2 * R2:4 * R2].rearrange("p k (m r) -> p k m r", r=RANK),
                    a_in[:, :, :, :].rearrange("p m k r -> p k m r"),
                    a_w[:, :, 0:2 * R2].rearrange("p k (m r) -> p k m r", r=RANK)).then_inc(al_ready, 1)

            with dve.Fori(0, S0 // RING - 2) as it:
                for u in range(RING):
                    stage0_step(it, u)
            for u in range(RING):
                stage0_step(S0 // RING - 2, u)
            split_a_gu(0)
            for u in range(RING):
                it = S0 // RING - 1
                if u % 2:
                    finish_x1(0, 2 * it + u // 2, u // 2, it)
                split_gu(0, 0, 0, u)

            with dve.Fori(0, BLOCKS) as blk:
                form_t_gu(blk)

                for seg, n in enumerate(SEGS):
                    def finish_act(it, u):
                        if u % 2 != (not is_half(seg, it, u)):
                            return
                        f, par = 2 * it + u // 2, u // 2
                        done = FT * blk + SEG_AT[seg] + f + 1
                        dve.wait_ge(act_ready, done - 1)
                        dve.wait_ge(silu_ready, done)
                        if is_half(seg, it, u):
                            nc.vector.tensor_tensor(work[0:HALF, 1, :], work[HALF:P, 0, :], gate_ps[par][HALF:P, :],
                                                    ALU.mult).then_inc(gu_read[par], 1)
                            dve.wait_ge(acth_ready, done)
                            sub(acth[HALF:P, f, :], work[0:HALF, 1, :], acth[0:HALF, f, :]).then_inc(act_ready, 1)
                            return
                        nc.vector.tensor_tensor(work[:, 1, :], work[:, 0, :], up_ps[par][:, :], ALU.mult
                                                ).then_inc(gu_read[par], 1)
                        dve.wait_ge(acth_ready, done)
                        sub(row(actl, f), work[:, 1, :], row(acth, f)).then_inc(act_ready, 1)
                        if seg == 0:
                            for half in range(2):
                                dve.wait_ge(x1l_ready[half], (HT // 2) * (blk + 1))
                            add(row(x1, f), row(x1h, f), row(x1l, f)).then_inc(x1_ready, 1)
                        if seg == X_SEG:
                            with dve.If(blk < BLOCKS - 1):
                                split_next_x(blk, f)

                    turns = 2 * n // RING - 1 - (seg == len(SEGS) - 1)
                    with dve.Fori(0, turns) as it:
                        for u in range(RING):
                            finish_act(it, u)
                            split_gu(blk, seg, it + 1, u)
                    for it in range(turns, 2 * n // RING - 1):
                        for u in range(RING):
                            finish_act(it, u)
                            split_gu(blk, seg, it + 1, u)
                    dve.wait_ge(adh_ready, 2 * (len(SEGS) * blk + seg + 1))
                    for q in range(2):
                        end = sub(ad_rows(n, 2 + q), ad_in[:, :, 0:n, :].rearrange("p b k r -> p k b r"), ad_rows(n, q))
                    end.then_inc(adl_ready, 1)

                    def last_act(u):
                        finish_act(2 * n // RING - 1, u)

                    def finish_down(h, slot, turns):
                        par = h % 2
                        dve.wait_ge(chunk_used[slot], turns + 1)
                        if seg:
                            dve.wait_ge(down_read[par], (3 * HT // 2) * blk + (HT // 2) * (seg - 1) + h // 2 + 1)
                        elif h == 0:
                            dve.wait_ge(x1_ready, HT * (blk + 1))
                        if seg < len(SEGS) - 1:
                            dst = x1[:, h, :]
                        else:
                            dve.wait_ge(out_stored[par], 16 * ((HT // 2) * blk + h // 2))
                            dst = stage[:, par, :]
                        add(dst, x1[:, h, :], down_ps[par][:, :]).then_inc(down_read[par], 1)

                    def downs(then):
                        for u in range(RING):
                            last_act(u)
                            if seg == len(SEGS) - 1 and u == RING // 2:
                                form_t_down(blk)
                                split_t_down(blk)
                            split_down(seg, u, u, turn(blk, DN_AT[seg], 0))
                        for u in range(RING):
                            finish_down(u, u, turn(blk, DN_AT[seg], 0))
                            split_down(seg, RING + u, u, turn(blk, DN_AT[seg], 1))
                        for u in range(RING):
                            finish_down(RING + u, u, turn(blk, DN_AT[seg], 1))
                            then(u)

                    if seg < len(SEGS) - 1:
                        downs(lambda u: split_gu(blk, seg + 1, 0, u))
                        continue

                    with dve.If(blk < BLOCKS - 1):
                        def matrix(p):
                            o, b = MIX[p]
                            if b < PAIR:
                                form_matrix(blk + 1, o // 2, PAIR * (o % 2) + b, p % RING)

                        def split(p):
                            o, b = MIX[p]
                            if b < PAIR:
                                split_matrix(*mixed(blk, p))
                            else:
                                split_down(seg, o, *mixed(blk, p))

                        def finish(p):
                            o, b = MIX[p]
                            if b == PAIR - 1:
                                finish_x1(blk + 1, o, o % 2, o // 2)
                            elif b == PAIR:
                                finish_down(o, *mixed(blk, p))

                        matrix(0)
                        for p in range(AHEAD):
                            last_act(p)
                            if p == AHEAD - 1:
                                form_t_down(blk)
                            matrix(p + 1)
                            split(p)
                        split_t_down(blk)
                        for p in range(AHEAD, len(MIX)):
                            finish(p - AHEAD)
                            if p + 1 < len(MIX):
                                matrix(p + 1)
                            split(p)
                        split_a_gu(blk + 1)
                        for u in range(RING):
                            finish(len(MIX) - AHEAD + u)
                            split_gu(blk + 1, 0, 0, u)
                    with dve.If(blk >= BLOCKS - 1):
                        downs(lambda u: None)

        @block.tensor
        def _(pe):
            mm = nc.tensor.matmul

            def three(dst, u, k, vh, vl, first, last, lora=None):
                w = slice(k * P, (k + 1) * P)
                mm(dst, hi[:, u, w], vh, start=first, stop=False)
                mm(dst, hi[:, u, w], vl, start=False, stop=False)
                if last and lora is not None:
                    mm(dst, b_w[0:TR, u, :], lora[:, :], start=False, stop=False)
                end = mm(dst, lo[:, u, w], vh, start=False, stop=last)
                if last:
                    end.then_inc(chunk_used[u], 1)

            def stage0(blk, it, u, slot, turns):
                b, par = u % 2, u // 2
                if b == 0:
                    pe.wait_ge(x1l_ready[par], (HT // 2) * blk + it)
                pe.wait_ge(lo_ready[slot], turns + 1)
                cols = slice(b * S, (b + 1) * S)
                for k in range(HT):
                    if isinstance(blk, int) and u == 0:
                        pe.wait_ge(xl_ready, k + 1)
                    three(gate_ps[par][:, cols], slot, k, xh[:, k, cols], xl[:, k, cols], k == 0, k == HT - 1)

            def down(blk, seg, par, half, slot, turns):
                n = SEGS[seg]
                pe.wait_ge(down_read[par], (3 * HT // 2) * blk + (HT // 2) * seg + half)
                pe.wait_ge(lo_ready[slot], turns + 1)
                half_tile = seg == len(SEGS) - 1
                dst = down_ps[par]
                for k in range(n - half_tile):
                    three(dst[:, :], slot, k, acth[:, k, :], actl[:, k, :], k == 0, k == n - 1)
                if half_tile:
                    w = slice((n - 1) * P, n * P)
                    mm(dst[:, :], hi[:, slot, w], acth[:, n - 1, :], start=False, stop=False)
                    pe.wait_ge(act_t_ready, blk + 1)
                    pe.wait_ge(td_ready, 2 * (blk + 1))
                    mm(dst[:, 0:S], lo[:, slot, w], act_t[:, 0:S], start=False, stop=False)
                    mm(dst[:, S:T], b_w[:, slot, :], act_t[:, S:T], start=False, stop=True
                       ).then_inc(chunk_used[slot], 1)

            with pe.Fori(0, S0 // RING) as it:
                for u in range(RING):
                    stage0(0, it, u, u, turn(0, 0, it))

            with pe.Fori(0, BLOCKS) as blk:
                pe.wait_ge(al_ready, blk + 1)
                for k in range(HT):
                    if k == 0:
                        pe.wait_ge(x1l_ready[0], (HT // 2) * (blk + 1))
                        pe.wait_ge(x1l_ready[1], (HT // 2) * (blk + 1) - 1)
                    if k == HT - 1:
                        pe.wait_ge(x1l_ready[1], (HT // 2) * (blk + 1))
                    mm(ta_ps[:, :], a_w[:, k, :], x1h[:, k, :], start=k == 0, stop=False)
                    end = mm(ta_ps[:, :], a_w[:, k, :], x1l[:, k, :], start=False, stop=k == HT - 1)
                end.then_inc(t_done, 1)

                for seg, n in enumerate(SEGS):
                    def gate_or_up(it, u):
                        par = u // 2
                        if u % 2 == 0:
                            pe.wait_ge(gu_read[par], (FT // 2) * blk + SEG_AT[seg] // 2 + it)
                        pe.wait_ge(lo_ready[u], turn(blk, GU_AT[seg], it) + 1)
                        dst, t = ((gate_ps[par], t_gate), (up_ps[par], t_up))[u % 2]
                        for k in range(HT):
                            if k == HT - 1 and seg == 0:
                                pe.wait_ge(t_hi, 2 * blk + u % 2 + 1)
                                pe.wait_ge(t_ready, 2 * blk + u % 2 + 1)
                            three(dst[:, :], u, k, x1h[:, k, :], x1l[:, k, :], k == 0, k == HT - 1, t)

                    def gate_and_up(it, u):
                        par, dst = u // 2, gate_ps[u // 2][:, :]
                        pe.wait_ge(gu_read[par], (FT // 2) * blk + SEG_AT[seg] // 2 + it)
                        for v in (u, u + 1):
                            pe.wait_ge(lo_ready[v], turn(blk, GU_AT[seg], it) + 1)
                        for k in range(HT):
                            w = slice(k * P, (k + 1) * P)
                            mm(dst, hi[:, u, w], x1h[:, k, :], start=k == 0, stop=False)
                            mm(dst, hi[:, u, w], x1l[:, k, :], start=False, stop=False)
                            if k < HT - 1:
                                mm(dst, lo[:, u, w], x1h[:, k, :], start=False, stop=False)
                        mm(dst, b_w[0:TR, u, :], t_gate[:, :], start=False, stop=False)
                        mm(dst, b_w[0:TR, u + 1, :], t_up[:, :], start=False, stop=False)
                        for b, v in enumerate((u + 1, u)):
                            q = slice(b * S, (b + 1) * S)
                            mm(dst[:, q], lo[:, u, w], x1h[:, HT - 1, q], start=False, stop=b == 1
                               ).then_inc(chunk_used[v], 1)

                    with pe.Fori(0, 2 * n // RING - (seg == len(SEGS) - 1)) as it:
                        for u in range(RING):
                            gate_or_up(it, u)
                    if seg == len(SEGS) - 1:
                        it = 2 * n // RING - 1
                        gate_or_up(it, 0)
                        gate_or_up(it, 1)
                        gate_and_up(it, 2)

                    def a_down_act():
                        pe.wait_ge(adl_ready, len(SEGS) * blk + seg + 1)
                        for k in range(n):
                            if k == 0 or k == n - 1:
                                pe.wait_ge(act_ready, FT * blk + SEG_AT[seg] + (n if k else n - 1))
                            start, stop = seg == 0 and k == 0, seg == len(SEGS) - 1 and k == n - 1
                            end = mm(td_ps[:, :], ad_w[:, k, :], acth[:, k, :], start=start, stop=stop)
                            if not stop:
                                end = mm(td_ps[:, :], ad_w[:, k, :], actl[:, k, :], start=False, stop=False)
                        if seg == len(SEGS) - 1:
                            end.then_inc(t_done, 1)

                    def downs():
                        with pe.Fori(0, HT // RING) as it:
                            for u in range(RING):
                                down(blk, seg, u % 2, 2 * it + u // 2, u, turn(blk, DN_AT[seg], it))

                    if seg < len(SEGS) - 1:
                        a_down_act()
                        downs()
                        continue
                    with pe.If(blk < BLOCKS - 1):
                        with pe.Fori(0, MIX_LOOPS) as loop:
                            for p, (o, b) in enumerate(MIX[:MIX_TURN]):
                                half = (HT // 4) * loop + o // 2
                                if b < PAIR:
                                    if p == 0:
                                        pe.wait_ge(gu_read[0], (FT // 2) * (blk + 1))
                                        pe.wait_ge(xl_ready, HT * (blk + 2))
                                    stage0(blk + 1, half, PAIR * (o % 2) + b, *mixed(blk, p, loop))
                                    if p == 0:
                                        with pe.If(loop < 1):
                                            a_down_act()
                                else:
                                    down(blk, seg, o % 2, half, *mixed(blk, p, loop))
                    with pe.If(blk >= BLOCKS - 1):
                        a_down_act()
                        downs()


def kernel(x, condB_coeff, itok_B_2_6, mask_Bx4096x4096_ik1, L0_cond_W, L0_cond_b, L1_cond_W_gate, L1_cond_W_up,
           L1_cond_W_down, L1_cond_A_gate, L1_cond_B_gate, L1_cond_A_up, L1_cond_B_up, L1_cond_A_down,
           L1_cond_B_down):
    import concourse.bacc as bacc
    from concourse.bass_utils import run_bass_kernel_spmd

    def pad_f(a, axis, before=0):
        zeros = np.zeros_like(np.take(a, range(HALF), axis))
        full, half = np.split(a, [F - HALF], axis)
        return np.concatenate([full, zeros, half] if before else [full, half, zeros], axis)

    def twice(a, axis):
        return np.concatenate([a, np.split(a, [F - HALF], axis)[1]], axis)

    def tiles(w, n_out, n_in):
        return w.reshape(n_out, P, n_in, P).transpose(0, 3, 2, 1).reshape(n_out, P, n_in * P)

    x, mask = np.asarray(x), np.asarray(mask_Bx4096x4096_ik1)
    wg, wu = (tiles(pad_f(np.asarray(w), 0), FT, HT) for w in (L1_cond_W_gate, L1_cond_W_up))
    for w in (wg, wu):
        w[-1, :, :H // 2] = w[-1].reshape(P, HT, P)[:, :, :HALF].reshape(P, H // 2)
    a_gate, a_up = (np.asarray(a)[0].reshape(ADAPTERS, RANK, HT, P).transpose(0, 3, 2, 1).reshape(ADAPTERS, P, -1)
                    for a in (L1_cond_A_gate, L1_cond_A_up))
    a_down = twice(np.asarray(L1_cond_A_down)[0], 2)
    a_down = a_down.reshape(ADAPTERS, RANK, FT, P).transpose(0, 3, 2, 1).reshape(ADAPTERS, P, -1)
    b_gate, b_up = (pad_f(np.asarray(b)[0].transpose(0, 2, 1), 2, before)
                    for b, before in ((L1_cond_B_gate, False), (L1_cond_B_up, True)))
    rows, cols = np.arange(2 * R2) % R2 // RANK, np.arange(T) // S
    arrays = {
        "x": x.reshape(BLOCKS, T, HT, P).transpose(0, 2, 3, 1).reshape(BLOCKS * HT, P, T),
        "mask": mask.reshape(BLOCKS, PAIR, HT, P, HT, P).transpose(0, 4, 1, 3, 2, 5).reshape(BLOCKS * S0, P, H),
        "coeff": np.broadcast_to(np.asarray(condB_coeff), (P, B)),
        "w0": tiles(np.asarray(L0_cond_W), HT, HT),
        "bias": np.asarray(L0_cond_b).reshape(HT, P).T,
        "wgu": np.stack([wg, wu], 1).reshape(2 * FT, P, H),
        "wd": tiles(twice(np.asarray(L1_cond_W_down), 1), HT, FT),
        "a_gate": a_gate, "a_up": a_up, "a_down": a_down,
        "b_gu": np.stack([b_gate, b_up], 2),
        "b_down": np.asarray(L1_cond_B_down)[0].transpose(0, 2, 1),
        "idx": np.asarray(itok_B_2_6).reshape(1, B),
        "ident": np.eye(P, dtype=np.float32),
        "own": np.where(rows[:, None] == cols[None, :], np.float32(LORA_SCALE), np.float32(0)),
        "pick_rows": np.repeat(np.float32([[0, 1], [1, -1]]), RANK, 0),
    }
    arrays = {f"in_{k}": np.ascontiguousarray(v) for k, v in arrays.items()}
    nc = bacc.Bacc("TRN2", target_bir_lowering=False, num_devices=1)
    args = [nc.dram_tensor(k, v.shape, mybir.dt.from_np(v.dtype), kind="ExternalInput").ap() for k, v in arrays.items()]
    args.append(nc.dram_tensor("out", (BLOCKS * HT, P, T), mybir.dt.float32, kind="ExternalOutput").ap())
    build(nc, *args)
    got = run_bass_kernel_spmd(nc, [arrays], core_ids=[0]).results[0]["out"]
    return got.reshape(BLOCKS, H, T).transpose(0, 2, 1).reshape(B, S, H)
```
